# Optimizing a Trainium2 kernel written in Bass

```python
import numpy as np
import jax
import jax.numpy as jnp

def _softmax(x, axis=-1):
    return jax.nn.softmax(x, axis=axis)

def _gelu(x):
    return jax.nn.gelu(x, approximate=True)

def _silu(x):
    return jax.nn.silu(x)

def _sigmoid(x):
    return jax.nn.sigmoid(x)

def _layernorm(x, axis=-1, eps=1e-05):
    m = jnp.mean(x, axis=axis, keepdims=True)
    v = jnp.var(x, axis=axis, keepdims=True)
    return (x - m) / jnp.sqrt(v + eps)

def _scatter_add(tgt, idx, src, axis=0):
    return tgt.at[idx].add(src)

def _segment_sum(src, seg, n):
    return jax.ops.segment_sum(src, seg, n)
kernel_name = 'mk_gnn_resnorm_d2_gnn_r32_9cefbe'

def setup_inputs(seed: int=0):
    np.random.seed(seed)
    _w = jnp.asarray

    def _rec_inputs():
        import jax
        import jax.numpy as jnp
        _gk = jax.random.key(seed)
        x = -0.0003713 + 1 * jax.random.normal(jax.random.fold_in(_gk, 1), (3125, 128), jnp.float32)
        _s = jax.random.randint(jax.random.fold_in(_gk, 2), (50000,), 0, 3125, jnp.int32)
        _d = jax.random.randint(jax.random.fold_in(_gk, 3), (50000,), 0, 3125, jnp.int32)
        _loop = jnp.arange(3125, dtype=jnp.int32)
        src = jnp.concatenate([_s, _d, _loop])
        dst = jnp.concatenate([_d, _s, _loop])
        _o = jnp.argsort(dst, stable=True)
        src = src[_o]
        dst = dst[_o]
        edge_attr_32 = 0.000189758 + 1.00013 * jax.random.normal(jax.random.fold_in(_gk, 12), (103125, 32), jnp.float32)
        edge_attr_64 = -8.16379e-05 + 0.999858 * jax.random.normal(jax.random.fold_in(_gk, 13), (103125, 64), jnp.float32)
        edge_weight = jax.random.uniform(jax.random.fold_in(_gk, 15), (103125,), jnp.float32, 0.0, 1)
        return (x, src, dst, edge_attr_32, edge_attr_64, edge_weight)
    x, src, dst, edge_attr_32, edge_attr_64, edge_weight = _rec_inputs()

    def _L0_gnn_setup():
        import jax, jax.numpy as jnp
        import numpy as np
        N_NODES = 3125
        N_EDGES = 50000
        D_IN = 128
        D_OUT = 128
        key = jax.random.key(seed)
        k1, k2, k3 = jax.random.split(key, 3)
        x = jax.random.normal(k1, (N_NODES, D_IN), dtype=jnp.float32)
        edge_index = jax.random.randint(k2, (2, N_EDGES), 0, N_NODES, dtype=jnp.int64)
        limit = float(np.sqrt(6.0 / (D_IN + D_OUT)))
        weight = jax.random.uniform(k3, (D_IN, D_OUT), dtype=jnp.float32, minval=-limit, maxval=limit)
        bias = jnp.zeros((D_OUT,), dtype=jnp.float32)
        return {'x': x, 'edge_index': edge_index, 'weight': weight, 'bias': bias}
    _L0_gnn_all = _L0_gnn_setup()
    _L0_gnn_in = {k: v for k, v in _L0_gnn_all.items() if k in ('weight', 'bias')}
    del _L0_gnn_all

    def _L1_gnn_setup():
        import jax, jax.numpy as jnp
        import numpy as np
        N_NODES = 3125
        N_EDGES = 50000
        D = 128
        H = 8
        HD = D // H
        RAD_IN, SPH_IN, HID = (64, 32, 256)
        AVG_NUM_NEIGHBORS = 16.0

        def _mlp(x, w0, b0, w1, b1):
            return jax.nn.silu(x @ w0 + b0) @ w1 + b1
        key = jax.random.key(seed)
        ks = jax.random.split(key, 16)

        def glorot(k, shape):
            fan_in, fan_out = (shape[0], shape[1])
            s = jnp.sqrt(2.0 / (fan_in + fan_out))
            return jax.random.normal(k, shape, dtype=jnp.float32) * s
        return {'node_feats': jax.random.normal(ks[0], (N_NODES, D), dtype=jnp.float32), 'edge_feats': jax.random.normal(ks[1], (N_EDGES, RAD_IN), dtype=jnp.float32), 'chi_scalar': jax.random.normal(ks[2], (N_EDGES, SPH_IN), dtype=jnp.float32), 'cutoffs': jax.random.uniform(ks[3], (N_EDGES,), dtype=jnp.float32), 'senders': jax.random.randint(ks[4], (N_EDGES,), 0, N_NODES, dtype=jnp.int32), 'receivers': jax.random.randint(ks[5], (N_EDGES,), 0, N_NODES, dtype=jnp.int32), 'rad_w0': glorot(ks[6], (RAD_IN, HID)), 'rad_b0': jnp.zeros((HID,), jnp.float32), 'rad_w1': glorot(ks[7], (HID, D)), 'rad_b1': jnp.zeros((D,), jnp.float32), 'sph_w0': glorot(ks[8], (SPH_IN, HID)), 'sph_b0': jnp.zeros((HID,), jnp.float32), 'sph_w1': glorot(ks[9], (HID, D)), 'sph_b1': jnp.zeros((D,), jnp.float32), 'wq': glorot(ks[10], (D, D)), 'wk': glorot(ks[11], (D, D)), 'wv': glorot(ks[12], (D, D))}
    _L1_gnn_all = _L1_gnn_setup()
    _L1_gnn_in = {k: v for k, v in _L1_gnn_all.items() if k in ('rad_w0', 'rad_b0', 'rad_w1', 'rad_b1', 'sph_w0', 'sph_b0', 'sph_w1', 'sph_b1', 'wq', 'wk', 'wv')}
    del _L1_gnn_all
    return {'x': x, 'src': src, 'dst': dst, 'edge_attr_32': edge_attr_32, 'edge_attr_64': edge_attr_64, 'edge_weight': edge_weight, 'L0_gnn_weight': _L0_gnn_in['weight'], 'L0_gnn_bias': _L0_gnn_in['bias'], 'L1_gnn_rad_w0': _L1_gnn_in['rad_w0'], 'L1_gnn_rad_b0': _L1_gnn_in['rad_b0'], 'L1_gnn_rad_w1': _L1_gnn_in['rad_w1'], 'L1_gnn_rad_b1': _L1_gnn_in['rad_b1'], 'L1_gnn_sph_w0': _L1_gnn_in['sph_w0'], 'L1_gnn_sph_b0': _L1_gnn_in['sph_b0'], 'L1_gnn_sph_w1': _L1_gnn_in['sph_w1'], 'L1_gnn_sph_b1': _L1_gnn_in['sph_b1'], 'L1_gnn_wq': _L1_gnn_in['wq'], 'L1_gnn_wk': _L1_gnn_in['wk'], 'L1_gnn_wv': _L1_gnn_in['wv']}

def reference(x, src, dst, edge_attr_32, edge_attr_64, edge_weight, L0_gnn_weight, L0_gnn_bias, L1_gnn_rad_w0, L1_gnn_rad_b0, L1_gnn_rad_w1, L1_gnn_rad_b1, L1_gnn_sph_w0, L1_gnn_sph_b0, L1_gnn_sph_w1, L1_gnn_sph_b1, L1_gnn_wq, L1_gnn_wk, L1_gnn_wv):
    import jax
    import jax.numpy as jnp

    def _L0_gnn_ref(x, edge_index, weight, bias):
        import jax, jax.numpy as jnp
        import numpy as np
        N_NODES = 3125
        N_EDGES = 50000
        D_IN = 128
        D_OUT = 128
        num_nodes = x.shape[0]
        src = edge_index[0]
        dst = edge_index[1]
        deg = jax.ops.segment_sum(jnp.ones_like(src, dtype=x.dtype), src, num_segments=num_nodes)
        deg_safe = jnp.where(deg > 0, deg, jnp.ones_like(deg))
        deg_inv_sqrt = jnp.where(deg > 0, jax.lax.rsqrt(deg_safe), jnp.zeros_like(deg))
        norm = deg_inv_sqrt[src] * deg_inv_sqrt[dst]
        h = x @ weight
        msgs = norm[:, None] * h[src]
        out = jax.ops.segment_sum(msgs, dst, num_segments=num_nodes)
        return out + bias

    def _L1_gnn_ref(node_feats, edge_feats, chi_scalar, cutoffs, senders, receivers, rad_w0, rad_b0, rad_w1, rad_b1, sph_w0, sph_b0, sph_w1, sph_b1, wq, wk, wv):
        import jax, jax.numpy as jnp
        import numpy as np
        N_NODES = 3125
        N_EDGES = 50000
        D = 128
        H = 8
        HD = D // H
        RAD_IN, SPH_IN, HID = (64, 32, 256)
        AVG_NUM_NEIGHBORS = 16.0

        def _mlp(x, w0, b0, w1, b1):
            return jax.nn.silu(x @ w0 + b0) @ w1 + b1
        n_nodes = node_feats.shape[0]
        w_ij = _mlp(edge_feats, rad_w0, rad_b0, rad_w1, rad_b1)
        w_ij = w_ij + _mlp(chi_scalar, sph_w0, sph_b0, sph_w1, sph_b1)
        w_ij = w_ij.reshape(-1, H, HD)
        q = (node_feats @ wq).reshape(-1, H, HD)[receivers]
        k = (node_feats @ wk).reshape(-1, H, HD)[senders]
        alpha = (q * w_ij * k).sum(axis=-1) / jnp.sqrt(jnp.float32(HD))
        alpha = alpha * cutoffs[:, None]
        v = (node_feats @ wv).reshape(-1, H, HD)[senders]
        out = jax.ops.segment_sum(alpha[..., None] * v, receivers, num_segments=n_nodes) / AVG_NUM_NEIGHBORS
        return out.reshape(n_nodes, D)
    edge_index = jnp.stack([src, dst])
    x = _layernorm(x + _L0_gnn_ref(x, edge_index, L0_gnn_weight, L0_gnn_bias), axis=-1)
    x = _layernorm(x + _L1_gnn_ref(x, edge_attr_64, edge_attr_32, edge_weight, src, dst, L1_gnn_rad_w0, L1_gnn_rad_b0, L1_gnn_rad_w1, L1_gnn_rad_b1, L1_gnn_sph_w0, L1_gnn_sph_b0, L1_gnn_sph_w1, L1_gnn_sph_b1, L1_gnn_wq, L1_gnn_wk, L1_gnn_wv), axis=-1)
    return x

_drawn_inputs = setup_inputs


def setup_inputs(seed=0):
    import zlib

    import numpy as np

    out = dict(_drawn_inputs(seed))
    spreads = {'L0_gnn_bias': (0.0, 0.1),
     'L1_gnn_rad_b0': (0.0, 0.553),
     'L1_gnn_rad_b1': (0.0, 0.358),
     'L1_gnn_sph_b0': (0.0, 0.582),
     'L1_gnn_sph_b1': (0.0, 0.339)}
    factors = {}
    for name, (base, spread) in spreads.items():
        noise = np.random.default_rng([zlib.crc32(name.encode()), seed]).standard_normal(out[name].shape)
        drawn = base * np.exp(spread * noise) if base else spread * noise
        out[name] = jnp.asarray(drawn.astype(out[name].dtype))
    for name, factor in factors.items():
        out[name] = (out[name] * factor).astype(out[name].dtype)
    return out
```

```python
from contextlib import ExitStack

import concourse.bass as bass
from concourse import mybir

P = 128
WIN = 64
TILES = 4
GE = P * TILES
HEADS, HD = 8, 16
RAD, SPH, HID = 64, 32, 256
EPS = 1e-5
AVG_NEIGHBORS = 16.0
UNROLL = 4
FIRST, LAST = 6, 4

F32 = mybir.dt.float32
F32R = mybir.dt.float32r
BF16 = mybir.dt.bfloat16
I32 = mybir.dt.int32
ALU = mybir.AluOpType
ACT = mybir.ActivationFunctionType
AX = mybir.AxisListType


class Step:

    def __init__(self, c, unroll=1, i=0, p=0, total=0):
        self.c, self.unroll, self.i, self.p, self.total = c, unroll, i, p, total

    @property
    def n(self):
        return self.i * self.unroll + self.c

    @property
    def tick(self):
        return self.p * self.total + self.n

    def slot(self, k):
        return self.c % k

    def round(self, k):
        per_pass = (self.total - self.slot(k) + k - 1) // k
        return self.p * per_pass + self.i * (self.unroll // k) + self.c // k

    def __add__(self, d):
        return Step(self.c + d, self.unroll, self.i, self.p, self.total)

    def __sub__(self, d):
        return self + (-d)


def run_steps(eng, total, first, unroll, last, step, p=0):
    turns = (total - first - last) // unroll
    assert first + turns * unroll + last == total and turns > 0
    for c in range(first):
        step(Step(c, p=p, total=total))
    with eng.Fori(0, turns) as i:
        for j in range(unroll):
            step(Step(first + j, unroll, i, p, total))
    for c in range(total - last, total):
        step(Step(c, p=p, total=total))


def at(eng, value):
    return value if isinstance(value, int) else eng.snap(value)


def ds(start, size):
    return bass.DynSlice(start, size)


def build(nc, x, x_pad, src_idx, src_e, dst_e, dst_row, dst_first, cut_e, rad_t, sph_t, w_l0, b_l0, rad_w0, rad_b0,
          rad_w1, rad_b1, sph_w0, sph_b0, sph_w1, sph_b1, wq, wk, wv, out):
    N, D = x.shape
    NB = x_pad.shape[1]
    NP = NB * P
    G = dst_row.shape[0]
    COLS = G * TILES
    WINDOWS = NP // WIN
    GP = G // 2
    assert NP <= WIN * WINDOWS and N + WIN <= NP + WIN - 1
    DEG_COLS = 8
    DEG_STEPS = COLS // DEG_COLS
    HI = NP // WIN

    with ExitStack() as ctx:
        def sb(name, shape, dt=F32):
            return ctx.enter_context(nc.sbuf_tensor(name, shape, dt))

        def sem(name):
            return ctx.enter_context(nc.semaphore(name))

        def sems(name, k):
            return [sem(f"{name}{i}") for i in range(k)]

        first_d = nc.dram_tensor("first_d", (1, G), F32).ap()
        relrow_d = nc.dram_tensor("relrow_d", (G, GE), BF16).ap()
        xs_d = nc.dram_tensor("xs_d", (NP, D), F32).ap()
        kv_d = nc.dram_tensor("kv_d", (NP, 2 * D), F32).ap()
        q_d = nc.dram_tensor("q_d", (NP + WIN, D), F32).ap()

        acc = sb("acc", [P, NP + WIN])
        nodes = sb("nodes", [P, NB, D])
        gath = sb("gath", [P, 4, TILES * 2 * D])
        idx = sb("idx", [P, 4, TILES], I32)
        onehot = sb("onehot", [P, 2, TILES, WIN])
        onehot_t = sb("onehot_t", [WIN, 2, GE])
        relrow_sb = sb("relrow_sb", [WIN, 4, GE], BF16)
        qwin = sb("qwin", [WIN, 4, D])
        xraw = sb("xraw", [P, 4, 2, GE])
        xsplit = sb("xsplit", [P, 2, 2, GE], F32R)
        hid = sb("hid", [P, 2, 4, GE])
        prod = sb("prod", [P, TILES, D])
        msg = sb("msg", [P, 2, TILES, D])
        red = sb("red", [P, TILES * HEADS])
        alpha = sb("alpha", [P, TILES * HEADS])
        rel0 = sb("rel0", [P, COLS])
        rel = sb("rel", [P, COLS])
        cut = sb("cut", [P, COLS])
        relrow0 = sb("relrow0", [GP, 2, GE])
        relrow = sb("relrow", [GP, 2, GE], BF16)
        base_f = sb("base_f", [P, G])
        base_i = sb("base_i", [1, G], I32)
        off = sb("off", [P, 1])
        passes_i = sb("passes_i", [1, 1], I32)
        iota_win = sb("iota_win", [P, WIN])
        iota_part = sb("iota_part", [P, 1])
        ident = sb("ident", [P, P])
        ones = sb("ones", [P, P])
        ones_bf = sb("ones_bf", [3, P], BF16)
        small = sb("small", [P, 16])
        dinv = sb("dinv", [P, NB])
        deg = sb("deg", [P, NB])
        w_l0_sb = sb("w_l0_sb", [P, D])
        b_l0_sb = sb("b_l0_sb", [P, D])
        wqkv = sb("wqkv", [P, 3 * D])
        w0_raw = sb("w0_raw", [P, 2, HID])
        w0_hi = sb("w0_hi", [P, 2, HID], F32R)
        w0_lo = sb("w0_lo", [P, 2, HID], F32R)
        b0 = sb("b0", [P, 4])
        w1 = sb("w1", [P, 4, D])
        b1_row = sb("b1_row", [1, 3, D])
        b1_parts = sb("b1_parts", [1, 3, TILES * D], BF16)
        b1_bf = sb("b1_bf", [3, TILES * D], BF16)
        stage = sb("stage", [P, 2, P])
        x_t = sb("x_t", [P, 2, P])
        qkv = sb("qkv", [P, 2, 3 * D])
        stats = sb("stats", [P, 2, 6])
        meanvar = sb("meanvar", [P, NB, 2])
        rstd = sb("rstd", [P, NB])
        src_i = sb("src_i", [P, COLS], I32)
        dig_i = sb("dig_i", [P, 2, COLS], I32)
        dig = sb("dig", [P, 2, COLS], BF16)
        iota_dig = sb("iota_dig", [P, WIN, DEG_COLS], BF16)
        iota_tmp = sb("iota_tmp", [P, WIN, DEG_COLS])
        lo_hot = sb("lo_hot", [P, 2, WIN, DEG_COLS], BF16)
        hi_hot = sb("hi_hot", [P, 2, HI, DEG_COLS], BF16)
        dst_ei = src_i
        dst_rowi = sb("dst_rowi", [GP, 2, GE], I32)
        dst_f = sb("dst_f", [P, COLS])

        xs_sb = gath[:, :, :].rearrange("p a b -> p (a b)")[:, 0:NB * D].rearrange("p (b f) -> p b f", b=NB)

        bank = [ctx.enter_context(nc.psum_tensor(f"bank{i}", [P, 512], F32)) for i in range(8)]
        hid_ps = bank[0:4]
        w_ps = bank[4:6]
        q_ps = bank[6]
        sum_ps = bank[7]

        s_dst = sem("s_dst")
        s_src = sem("s_src")
        s_wts = sem("s_wts")
        s_const = sem("s_const")
        s_first = sem("s_first")
        s_firstb = sem("s_firstb")
        s_pre = sem("s_pre")
        s_viol = sem("s_viol")
        s_hot = sem("s_hot")
        s_degmm = sem("s_degmm")
        s_degp = sem("s_degp")
        s_xs = sem("s_xs")
        s_b1 = sem("s_b1")
        s_wsplit = sem("s_wsplit")
        s_pass1 = sem("s_pass1")
        s_idx1 = sems("s_idx1_", 2)
        s_gath1 = sems("s_gath1_", 4)
        s_hot1 = sem("s_hot1")
        s_sum1 = sem("s_sum1")
        s_acc1 = sem("s_acc1")
        s_stage = sem("s_stage")
        s_conv = sem("s_conv")
        s_row = sem("s_row")
        s_bn = sem("s_bn")
        s_mv = sem("s_mv")
        s_rstd = sem("s_rstd")
        s_norm = sem("s_norm")
        s_tr = sem("s_tr")
        s_trc = sem("s_trc")
        s_proj = sem("s_proj")
        s_projc = sem("s_projc")
        s_table = sems("s_table", 2)
        s_go = sem("s_go")
        s_sp_pass = sem("s_sp_pass")
        s_pass2 = sem("s_pass2")
        s_relrow = sem("s_relrow")
        s_idx2 = sems("s_idx2_", 2)
        s_gath2 = sems("s_gath2_", 4)
        s_x = sems("s_x", 2)
        s_rr = sems("s_rr", 2)
        s_qw = sems("s_qw", 4)
        s_hi = sem("s_hi")
        s_lo = sem("s_lo")
        s_l1 = sem("s_l1")
        s_silu = sem("s_silu")
        s_w = sem("s_w")
        s_hott = sem("s_hott")
        s_q = sem("s_q")
        s_qk = sem("s_qk")
        s_qkw = sem("s_qkw")
        s_red = sem("s_red")
        s_al = sem("s_al")
        s_msg = sem("s_msg")
        s_sum2 = sem("s_sum2")
        s_acc2 = sem("s_acc2")
        s_fstage = sem("s_fstage")
        s_ftr = sem("s_ftr")
        s_frow = sem("s_frow")
        s_fbn = sem("s_fbn")
        s_fmv = sem("s_fmv")
        s_frstd = sem("s_frstd")
        s_fnorm = sem("s_fnorm")
        s_out = sem("s_out")

        WEIGHTS = 16 * 19
        TABLES = [32 * ((NB + 1) // 2) + 16, 32 * (NB // 2)]
        block = ctx.enter_context(nc.Block())

        def passes(eng):
            return eng.value_load(passes_i[0:1, 0:1], min_val=1, max_val=WINDOWS)


        @block.sync
        def _(sp):
            sp.dma_start(base_i[:, :], dst_first).then_inc(s_dst, 16)
            sp.dma_start(dst_ei[:, :], dst_e).then_inc(s_dst, 16)
            sp.dma_start(dst_rowi[:, :, :], dst_row.rearrange("(p j) e -> p j e", j=2)).then_inc(s_dst, 16)
            sp.dma_start(nodes[:, :, :], x_pad).then_inc(s_wts, 16)
            sp.dma_start(cut[:, :], cut_e).then_inc(s_wts, 16)
            sp.dma_start(w_l0_sb[:, :], w_l0).then_inc(s_wts, 16)
            sp.dma_start(b_l0_sb[:, :], b_l0.partition_broadcast(P)).then_inc(s_wts, 16)
            for j, w in enumerate((wq, wk, wv)):
                sp.dma_start(wqkv[:, j * D:(j + 1) * D], w).then_inc(s_wts, 16)
            for j in range(2):
                sp.dma_start(w0_raw[j * RAD:(j + 1) * RAD, 0, :], rad_w0).then_inc(s_wts, 16)
            for j in range(4):
                sp.dma_start(w0_raw[j * SPH:(j + 1) * SPH, 1, :], sph_w0).then_inc(s_wts, 16)
            for j, b in enumerate((rad_b0, sph_b0)):
                sp.dma_start(b0[:, 2 * j:2 * j + 2], b.rearrange("(c p) -> p c", p=P),
                             allow_slow_non_contiguous=True).then_inc(s_wts, 16)
            for j, w in enumerate((rad_w1, sph_w1)):
                sp.dma_start(w1[:, 2 * j:2 * j + 2, :], w.rearrange("(c p) f -> p c f", p=P)).then_inc(s_wts, 16)
            for j, b in enumerate((rad_b1, sph_b1)):
                sp.dma_start(b1_row[0:1, j, :], b.rearrange("(o f) -> o f", o=1)).then_inc(s_wts, 16)
            sp.wait_ge(s_pre, 1)
            sp.dma_start(first_d, base_f[0:1, :]).then_inc(s_first, 16)
            sp.wait_ge(s_first, 16)
            sp.dma_start(base_f[:, :], first_d[0, :].partition_broadcast(P)).then_inc(s_firstb, 16)
            sp.wait_ge(s_pre, 2)
            sp.dma_start(src_i[:, :], src_e).then_inc(s_src, 16)
            sp.wait_ge(s_pre, PRE.b1)
            sp.dma_start(b1_bf[:, :], b1_parts[0:1, :, :]).then_inc(s_b1, 16)
            sp.wait_ge(s_pre, PRE.xs)
            sp.dma_start(xs_d.rearrange("(b p) f -> p b f", p=P), xs_sb).then_inc(s_xs, 16)

            n_pass = passes(sp)

            def load_idx1(s):
                first = at(sp, s.n * 2)
                if not (isinstance(s.n, int) and s.n < 2):
                    for j in range(2):
                        g = 2 * s.slot(2) + j
                        sp.wait_ge(s_gath1[g], (s - 2).round(2) * 16 * TILES + 16 * TILES)
                sp.dma_start(idx[:, 2 * s.slot(2):2 * s.slot(2) + 2, :],
                             src_idx[:, ds(first, 2), :]).then_inc(s_idx1[s.slot(2)], 16)

            with sp.Fori(0, n_pass) as p:
                sp.wait_ge(s_acc1, p * G)
                run_steps(sp, G // 2, 3, 2, 2, load_idx1, p)

            def store_tables(s):
                node = at(sp, s.n * P)
                sp.wait_ge(s_projc, s.n + 1)
                sp.dma_start(kv_d[ds(node, P), :], qkv[:, s.slot(2), D:3 * D]).then_inc(s_table[s.slot(2)], 16)
                sp.dma_start(q_d[ds(node, P), :], qkv[:, s.slot(2), 0:D]).then_inc(s_table[s.slot(2)], 16)

            run_steps(sp, NB, 3, 2, 2, store_tables)
            sp.dma_start(q_d[NP:NP + WIN, :], qkv[0:WIN, 0, 0:D]).then_inc(s_table[0], 16)
            for j in range(2):
                sp.wait_ge(s_table[j], TABLES[j])

            def load_pair(s):
                a, h = s.slot(2), slice(2 * s.slot(2), 2 * s.slot(2) + 2)
                later = not (isinstance(s.n, int) and s.n < 2)
                first, edge = at(sp, s.n * 2), at(sp, s.n * 2 * GE)
                if later:
                    sp.wait_ge(s_lo, ((s - 2).tick + 1) * 2)
                for j in range(2):
                    sp.dma_start(xraw[j * RAD:(j + 1) * RAD, h, 0, :],
                                 rad_t[:, ds(edge, 2 * GE)].rearrange("p (g e) -> p g e", g=2)).then_inc(s_x[a], 16)
                for j in range(4):
                    sp.dma_start(xraw[j * SPH:(j + 1) * SPH, h, 1, :],
                                 sph_t[:, ds(edge, 2 * GE)].rearrange("p (g e) -> p g e", g=2)).then_inc(s_x[a], 16)
                if later:
                    sp.wait_ge(s_hott, ((s - 2).tick + 1) * 2)
                    for j in range(2):
                        g = 2 * a + j
                        sp.wait_ge(s_gath2[g], (s - 2).round(2) * 16 * TILES + 16 * TILES)
                sp.dma_start(idx[:, h, :], src_idx[:, ds(first, 2), :]).then_inc(s_idx2[a], 16)
                sp.dma_start(relrow_sb[:, h, :],
                             relrow_d[ds(first, 2), :].partition_broadcast(WIN)).then_inc(s_rr[a], 16)
                for j in range(2):
                    base = sp.value_load(base_i[0:1, ds(s.n * 2 + j, 1)], min_val=0, max_val=NP - 1)
                    if later:
                        sp.wait_ge(s_q, s.tick * 2 + j - 3)
                    sp.dma_start(qwin[:, 2 * a + j, :], q_d[ds(base, WIN), :]).then_inc(s_qw[2 * a + j], 16)

            with sp.Fori(0, n_pass) as p:
                sp.wait_ge(s_pass2, p * 4 + 3)
                sp.dma_start(relrow_d.rearrange("(p j) e -> p j e", j=2), relrow[:, :, :]).then_inc(s_relrow, 16)
                sp.wait_ge(s_relrow, p * 16 + 16)
                run_steps(sp, G // 2, 3, 2, 2, load_pair, p)
                sp.wait_ge(s_acc2, p * G + G)
                sp.sem_inc(s_sp_pass, 1)

            full = N // P
            sp.wait_ge(s_fnorm, 2)
            sp.dma_start(out[0:full * P, :].rearrange("(b p) f -> p b f", p=P), nodes[:, 0:full, :]).then_inc(s_out, 16)
            sp.dma_start(out[full * P:N, :], nodes[0:N - full * P, full, :]).then_inc(s_out, 16)
            sp.wait_ge(s_out, 32)
            sp.wait_ge(s_xs, 16)

        @block.gpsimd
        def _(pool):
            pool.iota(iota_tmp[:, :, :], [[1, WIN], [0, DEG_COLS]], base=0, channel_multiplier=0,
                      allow_small_or_imprecise_dtypes=True).then_inc(s_const, 1)
            pool.iota(iota_win[:, :], [[1, WIN]], base=0, channel_multiplier=0,
                      allow_small_or_imprecise_dtypes=True).then_inc(s_const, 1)
            pool.iota(iota_part[:, :], [[0, 1]], base=0, channel_multiplier=1,
                      allow_small_or_imprecise_dtypes=True).then_inc(s_const, 1)
            pool.memset(ones[:, :], 1.0).then_inc(s_const, 1)
            pool.memset(ones_bf[:, :], 1.0).then_inc(s_const, 1)
            pool.memset(acc[:, :], 0.0).then_inc(s_const, 1)
            pool.memset(ident[:, :], 0.0).then_inc(s_const, 1)
            pool.wait_ge(s_const, 7)
            pool.affine_select(out=ident[:, :], in_=ident[:, :], compare_op=ALU.not_equal, fill=1.0, base=0,
                               pattern=[[-1, P]], channel_multiplier=1).then_inc(s_const, 1)
            pool.wait_ge(s_pre, PRE.passes)
            n_pass = passes(pool)
            pool.wait_ge(s_xs, 16)

            def gather1(s):
                k = s.slot(4)
                pool.wait_ge(s_idx1[k // 2], s.round(4) * 16 + 16)
                if not (isinstance(s.n, int) and s.n < 4):
                    pool.wait_ge(s_sum1, (s - 4).tick + 1)
                pool.sem_inc(s_go, 1)
                for t in range(TILES):
                    pool.indirect_dma_start(gath[:, k, t * D:(t + 1) * D], None, xs_d,
                                            bass.IndirectOffsetOnAxis(ap=idx[:, k, t:t + 1], axis=0)
                                            ).then_inc(s_gath1[k], 16)

            with pool.Fori(0, n_pass) as p:
                run_steps(pool, G, FIRST, UNROLL, LAST, gather1, p)
                pool.wait_ge(s_acc1, p * G + G)

            for j in range(2):
                pool.wait_ge(s_table[j], TABLES[j])

            def gather2(s):
                k = s.slot(4)
                pool.wait_ge(s_idx2[k // 2], s.round(4) * 16 + 16)
                if not (isinstance(s.n, int) and s.n < 4):
                    pool.wait_ge(s_msg, (s - 4).tick + 1)
                pool.sem_inc(s_go, 1)
                for t in range(TILES):
                    pool.indirect_dma_start(gath[:, k, t * 2 * D:(t + 1) * 2 * D], None, kv_d,
                                            bass.IndirectOffsetOnAxis(ap=idx[:, k, t:t + 1], axis=0)
                                            ).then_inc(s_gath2[k], 16)

            with pool.Fori(0, n_pass) as p:
                run_steps(pool, G, FIRST, UNROLL, LAST, gather2, p)
                pool.wait_ge(s_acc2, p * G + G)

        @block.scalar
        def _(act):
            act.wait_ge(s_pre, PRE.passes)
            n_pass = passes(act)
            act.wait_ge(s_pre, PRE.deg)
            act.activation(dinv[:, :], dinv[:, :], ACT.Sqrt).then_inc(s_degp, 1)
            act.wait_ge(s_rstd, 1)
            act.activation(rstd[:, :], rstd[:, :], ACT.Sqrt).then_inc(s_rstd, 1)

            def evacuate(s):
                b = s.slot(2)
                act.wait_ge(s_tr, s.n + 1)
                if not (isinstance(s.n, int) and s.n < 2):
                    act.wait_ge(s_proj, (s - 2).n + 1)
                act.activation(x_t[:, b, :], bank[2 + b][:, 0:P], ACT.Copy).then_inc(s_trc, 1)
                act.wait_ge(s_proj, s.n + 1)
                if not (isinstance(s.n, int) and s.n < 2):
                    act.wait_ge(s_table[b], (s - 2).round(2) * 32 + 32)
                act.mul(qkv[:, b, 0:D], bank[4 + b][:, 0:D], 1.0 / (HD ** 0.5 * AVG_NEIGHBORS))
                act.activation(qkv[:, b, D:3 * D], bank[4 + b][:, D:3 * D], ACT.Copy).then_inc(s_projc, 1)

            run_steps(act, NB, 3, 2, 2, evacuate)

            act.wait_ge(s_wts, WEIGHTS)

            def split_hi(s):
                act.wait_ge(s_x[s.slot(4) // 2], s.round(4) * 96 + 96)
                if not (isinstance(s.n, int) and s.n < 2):
                    act.wait_ge(s_l1, ((s - 2).tick + 1) * 4)
                act.activation(xsplit[:, s.slot(2), :, :], xraw[:, s.slot(4), :, :], ACT.Copy).then_inc(s_hi, 1)

            def silu(s):
                for c in range(4):
                    act.wait_ge(s_l1, s.tick * 4 + c + 1)
                    if c == 0 and not (isinstance(s.n, int) and s.n < 2):
                        act.wait_ge(s_w, (s - 2).tick + 1)
                    act.activation(hid[:, s.slot(2), c, :], hid_ps[c][:, :], ACT.Silu,
                                   bias=b0[:, c:c + 1]).then_inc(s_silu, 1)

            def step(s):
                if isinstance(s.n, int) and s.n == 0:
                    split_hi(s)
                    split_hi(s + 1)
                    silu(s)
                if not (isinstance(s.n, int) and s.n >= G - 2):
                    split_hi(s + 2)
                if not (isinstance(s.n, int) and s.n >= G - 1):
                    silu(s + 1)

            with act.Fori(0, n_pass) as p:
                run_steps(act, G, FIRST, UNROLL, LAST, step, p)
                act.wait_ge(s_acc2, p * G + G)
            act.wait_ge(s_frstd, 1)
            act.activation(rstd[:, :], rstd[:, :], ACT.Sqrt).then_inc(s_frstd, 1)

        @block.tensor
        def _(pe):
            pe.wait_ge(s_const, 8)
            pe.wait_ge(s_pre, PRE.viol)
            pe.matmul(bank[0][:, 0:1], ones[:, :], small[:, 2:3], start=True, stop=True).then_inc(s_viol, 1)

            def count(s):
                b = s.slot(2)
                pe.wait_ge(s_hot, s.n + 1)
                for t in range(DEG_COLS):
                    one = isinstance(s.n, int)
                    mm = pe.matmul(bank[1][0:WIN, 0:HI], lo_hot[:, b, :, t], hi_hot[:, b, :, t],
                                   start=(one and s.n == 0 and t == 0),
                                   stop=(one and s.n == DEG_STEPS - 1 and t == DEG_COLS - 1),
                                   skip_group_check=True)
                mm.then_inc(s_degmm, 1)

            run_steps(pe, DEG_STEPS, 3, 2, 2, count)
            n_pass = passes(pe)

            def sum1(s):
                k = s.slot(4)
                pe.wait_ge(s_gath1[k], s.round(4) * 16 * TILES + 16 * TILES)
                pe.wait_ge(s_hot1, s.tick + 1)
                if not (isinstance(s.n, int) and s.n < 2):
                    pe.wait_ge(s_acc1, (s - 2).tick + 1)
                for t in range(TILES):
                    mm = pe.matmul(bank[s.slot(2)][:, 0:WIN], gath[:, k, t * D:(t + 1) * D],
                                   onehot[:, s.slot(2), t, :], start=(t == 0), stop=(t == TILES - 1))
                mm.then_inc(s_sum1, 1)

            with pe.Fori(0, n_pass) as p:
                run_steps(pe, G, FIRST, UNROLL, LAST, sum1, p)
                pe.wait_ge(s_acc1, p * G + G)

            pe.wait_ge(s_wts, WEIGHTS)

            def convolve(s):
                b = s.slot(2)
                pe.wait_ge(s_stage, s.n + 1)
                if not (isinstance(s.n, int) and s.n < 2):
                    pe.wait_ge(s_row, (s - 2).n + 1)
                pe.matmul(bank[b][:, 0:D], stage[:, b, :], w_l0_sb[:, :], start=True, stop=True).then_inc(s_conv, 1)

            run_steps(pe, NB, 3, 2, 2, convolve)

            def project(s):
                b = s.slot(2)
                pe.wait_ge(s_trc, s.n + 1)
                if not (isinstance(s.n, int) and s.n < 2):
                    pe.wait_ge(s_projc, (s - 2).n + 1)
                pe.matmul(bank[4 + b][:, 0:3 * D], x_t[:, b, :], wqkv[:, :], start=True, stop=True).then_inc(s_proj, 1)

            def transpose_project(s):
                b = s.slot(2)
                pe.wait_ge(s_norm, s.n + 1)
                if not (isinstance(s.n, int) and s.n < 2):
                    pe.wait_ge(s_trc, (s - 2).n + 1)
                pe.transpose(bank[2 + b][:, 0:P], stage[:, b, :], ident[:, :]).then_inc(s_tr, 1)
                if not (isinstance(s.n, int) and s.n == 0):
                    project(s - 1)

            run_steps(pe, NB, 3, 2, 2, transpose_project)
            project(Step(NB - 1))
            pe.wait_ge(s_projc, NB)
            pe.wait_ge(s_wsplit, 4)
            pe.wait_ge(s_b1, 16)

            def layer1(s):
                b = s.slot(2)
                pe.wait_ge(s_lo, s.tick + 1)
                for c in range(4):
                    if not (isinstance(s.n, int) and s.n < 1):
                        pe.wait_ge(s_silu, (s - 1).tick * 4 + c + 1)
                    m, cols = c // 2, slice((c % 2) * P, (c % 2) * P + P)
                    mm = pe.matmul(hid_ps[c][:, :], w0_hi[:, m, cols], xsplit[:, b, m, :], start=True, stop=(m == 1))
                    if m == 0:
                        mm = pe.matmul(hid_ps[c][:, :], w0_lo[:, m, cols], xsplit[:, b, m, :], start=False, stop=True)
                    mm.then_inc(s_l1, 1)

            def layer2(s):
                b = s.slot(2)
                if not (isinstance(s.n, int) and s.n < 2):
                    pe.wait_ge(s_qkw, (s - 2).tick + 1)
                pe.matmul(w_ps[b][:, :], ones_bf[:, :], b1_bf[:, :], start=True, stop=False, skip_group_check=True)
                for c in range(4):
                    pe.wait_ge(s_silu, s.tick * 4 + c + 1)
                    for t in range(TILES):
                        mm = pe.matmul(w_ps[b][:, t * D:(t + 1) * D], hid[:, b, c, t * P:(t + 1) * P], w1[:, c, :],
                                       start=False, stop=(c == 3), skip_group_check=True)
                mm.then_inc(s_w, 1)

            def expand_q(s):
                b = s.slot(2)
                pe.wait_ge(s_hott, s.tick + 1)
                pe.wait_ge(s_qw[s.slot(4)], s.round(4) * 16 + 16)
                if not (isinstance(s.n, int) and s.n < 1):
                    pe.wait_ge(s_qk, (s - 1).tick + 1)
                for t in range(TILES):
                    mm = pe.matmul(q_ps[:, t * D:(t + 1) * D], onehot_t[:, b, t * P:(t + 1) * P], qwin[:, s.slot(4), :],
                                   start=True, stop=True, skip_group_check=True)
                mm.then_inc(s_q, 1)

            def sum2(s):
                b = s.slot(2)
                pe.wait_ge(s_msg, s.tick + 1)
                if not (isinstance(s.n, int) and s.n < 1):
                    pe.wait_ge(s_acc2, (s - 1).tick + 1)
                for t in range(TILES):
                    mm = pe.matmul(sum_ps[:, 0:WIN], msg[:, b, t, :], onehot[:, b, t, :],
                                   start=(t == 0), stop=(t == TILES - 1))
                mm.then_inc(s_sum2, 1)

            def step(s):
                static = isinstance(s.n, int)
                if static and s.n == 0:
                    layer1(s)
                if not (static and s.n == G - 1):
                    layer1(s + 1)
                layer2(s)
                expand_q(s)
                if not (static and s.n == 0):
                    sum2(s - 1)
                if static and s.n == G - 1:
                    sum2(s)

            with pe.Fori(0, n_pass) as p:
                run_steps(pe, G, FIRST, UNROLL, LAST, step, p)
                pe.wait_ge(s_acc2, p * G + G)

            def transpose_back(s):
                b = s.slot(2)
                pe.wait_ge(s_fstage, s.n + 1)
                if not (isinstance(s.n, int) and s.n < 2):
                    pe.wait_ge(s_frow, (s - 2).n + 1)
                pe.transpose(bank[b][:, 0:P], stage[:, b, :], ident[:, :]).then_inc(s_ftr, 1)

            run_steps(pe, NB, 3, 2, 2, transpose_back)

        @block.vector
        def _(dve):
            done = [0]

            def pre(ins):
                done[0] += 1
                ins.then_inc(s_pre, 1)
                return done[0]

            def pre_wait(v):
                dve.wait_ge(s_pre, v)

            def group_bcast(row):
                return row.unsqueeze(2).to_broadcast([P, G, TILES])

            def by_group(t):
                return t.rearrange("p (g t) -> p g t", t=TILES)

            dve.wait_ge(s_dst, 48)
            pre(dve.tensor_copy(base_f[0:1, :], base_i[:, :]))
            v_dst = pre(dve.tensor_copy(dst_f[:, :], dst_ei[:, :]))
            v_row = pre(dve.tensor_copy(relrow0[:, :, :], dst_rowi[:, :, :]))
            dve.wait_ge(s_firstb, 16)
            pre_wait(v_dst)
            v = pre(dve.tensor_tensor(by_group(rel[:, :]), by_group(dst_f[:, :]), group_bcast(base_f[:, :]), ALU.subtract))
            pre_wait(v)
            pre(dve.tensor_reduce(small[:, 0:1], rel[:, :], AX.X, ALU.max))
            v = pre(dve.tensor_reduce(small[:, 1:2], rel[:, :], AX.X, ALU.min))
            pre_wait(v)
            v = pre(dve.tensor_scalar(small[:, 0:1], small[:, 0:1], WIN - 0.5, None, ALU.is_gt))
            pre_wait(v)
            v = pre(dve.scalar_tensor_tensor(out=small[:, 2:3], in0=small[:, 1:2], scalar=-0.5, in1=small[:, 0:1],
                                             op0=ALU.is_lt, op1=ALU.add))
            assert v == PRE.viol, v
            dve.wait_ge(s_viol, 1)
            v = pre(dve.tensor_scalar(small[:, 3:4], bank[0][:, 0:1], 0.5, None, ALU.is_lt))
            pre_wait(v)
            v = pre(dve.tensor_scalar(passes_i[:, :], small[0:1, 3:4], float(1 - WINDOWS), float(WINDOWS),
                                      ALU.mult, ALU.add))
            assert v == PRE.passes, v
            v = pre(dve.tensor_scalar(base_f[:, :], base_f[:, :], small[:, 3:4], None, ALU.mult))
            pre(dve.tensor_scalar(small[0:GP, 4:5], relrow0[:, 0, 0:1], small[0:GP, 3:4], None, ALU.mult))
            v_rb = pre(dve.tensor_scalar(small[0:GP, 5:6], relrow0[:, 1, 0:1], small[0:GP, 3:4], None, ALU.mult))
            pre_wait(v)
            pre(dve.tensor_tensor(by_group(rel0[:, :]), by_group(dst_f[:, :]), group_bcast(base_f[:, :]), ALU.subtract))
            pre_wait(v_rb)
            for j in range(2):
                pre(dve.tensor_scalar(relrow0[:, j, :], relrow0[:, j, :], small[0:GP, 4 + j:5 + j], None, ALU.subtract))

            dve.wait_ge(s_const, 8)
            pre(dve.tensor_copy(iota_dig[:, :, :], iota_tmp[:, :, :]))
            dve.wait_ge(s_src, 16)
            pre(dve.tensor_scalar(dig_i[:, 0, :], src_i[:, :], WIN - 1, None, ALU.bitwise_and))
            v = pre(dve.tensor_scalar(dig_i[:, 1, :], src_i[:, :], WIN.bit_length() - 1, None, ALU.logical_shift_right))
            pre_wait(v)
            v = pre(dve.tensor_copy(dig[:, :, :], dig_i[:, :, :]))
            pre_wait(v)

            def hots(s):
                b = s.slot(2)
                if not (isinstance(s.n, int) and s.n < 2):
                    dve.wait_ge(s_degmm, (s - 2).n + 1)
                for j, (hot, w) in enumerate(((lo_hot, WIN), (hi_hot, HI))):
                    digits = dig[:, j, ds(s.n * DEG_COLS, DEG_COLS)].unsqueeze(1).to_broadcast([P, w, DEG_COLS])
                    last = dve.tensor_tensor(hot[:, b, :, :], digits, iota_dig[:, 0:w, :], ALU.is_equal)
                last.then_inc(s_hot, 1)

            run_steps(dve, DEG_STEPS, 3, 2, 2, hots)

            dve.wait_ge(s_wts, WEIGHTS)
            dve.tensor_copy(w0_hi[:, :, :], w0_raw[:, :, :]).then_inc(s_wsplit, 1)
            dve.wait_ge(s_wsplit, 1)
            dve.tensor_tensor(w0_lo[:, :, :], w0_raw[:, :, :], w0_hi[:, :, :].bitcast(F32), ALU.subtract).then_inc(s_wsplit, 1)
            dve.wait_ge(s_wsplit, 2)
            for j in (1, 3):
                dve.tensor_tensor(w0_hi[j * SPH:(j + 1) * SPH, 1, :], w0_raw[j * SPH:(j + 1) * SPH, 1, :],
                                  w0_hi[j * SPH:(j + 1) * SPH, 1, :].bitcast(F32), ALU.subtract).then_inc(s_wsplit, 1)
            v = pre(dve.tensor_tensor(b1_row[:, 2, :], b1_row[:, 0, :], b1_row[:, 1, :], ALU.add))
            for part in range(3):
                pre_wait(v)
                v = pre(dve.tensor_copy(b1_parts[:, part, :].rearrange("p (t f) -> p t f", t=TILES),
                                        b1_row[:, 2:3, :].to_broadcast([1, TILES, D])))
                if part < 2:
                    pre_wait(v)
                    v = pre(dve.tensor_tensor(b1_row[:, 2, :], b1_row[:, 2, :], b1_parts[:, part, 0:D], ALU.subtract))
            assert v == PRE.b1, v

            dve.wait_ge(s_degmm, DEG_STEPS)
            by_half = bank[1][0:WIN, 0:HI].rearrange("p (b h) -> p h b", h=2)
            pre(dve.tensor_copy(deg[0:WIN, :], by_half[:, 0, :]))
            v = pre(dve.tensor_copy(deg[WIN:P, :], by_half[:, 1, :]))
            pre_wait(v)
            v = pre(dve.tensor_scalar(dinv[:, :], deg[:, :], 1.0, None, ALU.max))
            assert v == PRE.deg, v
            dve.wait_ge(s_degp, 1)
            v = pre(dve.reciprocal(dinv[:, :], dinv[:, :]))
            pre_wait(v)
            v = pre(dve.scalar_tensor_tensor(out=dinv[:, :], in0=deg[:, :], scalar=0.5, in1=dinv[:, :],
                                             op0=ALU.is_gt, op1=ALU.mult))
            pre_wait(v)
            v = pre(dve.tensor_tensor(xs_sb, nodes[:, :, :], dinv[:, :].unsqueeze(2).to_broadcast([P, NB, D]), ALU.mult))
            assert v == PRE.xs, v
            pre_wait(v)
            v_xb = pre(dve.tensor_tensor(nodes[:, :, :], nodes[:, :, :],
                                         b_l0_sb[:, :].unsqueeze(1).to_broadcast([P, NB, D]), ALU.add))

            v = pre(dve.memset(off[:, :], 0.0))
            pre_wait(v)
            n_pass = passes(dve)

            def start_pass(p, s_pass, rows):
                dve.tensor_scalar(rel[:, :], rel0[:, :], off[:, 0:1], None, ALU.subtract).then_inc(s_pass, 1)
                if rows:
                    dve.tensor_scalar(relrow[:, :, :], relrow0[:, :, :], off[0:GP, 0:1], None,
                                      ALU.subtract).then_inc(s_pass, 1)
                else:
                    dve.tensor_copy(small[:, 6:7], off[:, 0:1]).then_inc(s_pass, 1)
                dve.tensor_scalar(base_i[:, :], base_f[0:1, :], off[0:1, 0:1], None, ALU.add).then_inc(s_pass, 1)
                dve.wait_ge(s_pass, p * 4 + 3)
                dve.tensor_scalar(off[:, :], off[:, :], float(WIN), None, ALU.add).then_inc(s_pass, 1)
                dve.wait_ge(s_pass, p * 4 + 4)

            def one_hot(s):
                at = rel[:, ds(s.n * TILES, TILES)].unsqueeze(2).to_broadcast([P, TILES, WIN])
                nodes_in = iota_win[:, :].unsqueeze(1).to_broadcast([P, TILES, WIN])
                return dve.tensor_tensor(onehot[:, s.slot(2), :, :], at, nodes_in, ALU.is_equal)

            bases = [None] * UNROLL

            def base_of(s):
                if isinstance(s.n, int):
                    return dve.value_load(base_i[0:1, s.n:s.n + 1], min_val=0, max_val=NP - 1)
                j = s.c + 1 - FIRST
                if j == 0:
                    _, bases[:] = nc.values_load_multi_w_load_instructions(
                        base_i[0:1, ds(s.n, UNROLL)], engines=[mybir.EngineType.DVE], min_val=0, max_val=NP - 1,
                        skip_runtime_bounds_check_because="base_i holds node numbers")
                return bases[j]

            def add_window(s, ps, s_sum, s_acc, first):
                base = base_of(s)
                dve.wait_ge(s_sum, s.tick + 1)
                if not first:
                    dve.wait_ge(s_acc, s.tick)
                dve.tensor_tensor(acc[:, ds(base, WIN)], acc[:, ds(base, WIN)], ps[:, 0:WIN], ALU.add).then_inc(s_acc, 1)

            def step1(s):
                static = isinstance(s.n, int)
                if not (static and s.n < 2):
                    dve.wait_ge(s_sum1, (s - 2).tick + 1)
                one_hot(s).then_inc(s_hot1, 1)
                if not (static and s.n == 0):
                    add_window(s - 1, bank[(s - 1).slot(2)], s_sum1, s_acc1, static and s.n == 1)
                if static and s.n == G - 1:
                    add_window(s, bank[s.slot(2)], s_sum1, s_acc1, False)

            with dve.Fori(0, n_pass) as p:
                start_pass(p, s_pass1, False)
                run_steps(dve, G, FIRST, UNROLL, LAST, step1, p)
                dve.wait_ge(s_acc1, p * G + G)

            def stage_block(s, s_stage, s_used):
                if not (isinstance(s.n, int) and s.n < 2):
                    dve.wait_ge(s_used, (s - 2).n + 1)
                dve.tensor_copy(stage[:, s.slot(2), :], acc[:, ds(s.n * P, P)]).then_inc(s_stage, 1)

            def statistics(s, s_row, s_bn, s_mv):
                dve.wait_ge(s_row, s.n + 1)
                dve.bn_stats(stats[:, s.slot(2), :], nodes[:, ds(s.n, 1), :].rearrange("p o f -> p (o f)")).then_inc(s_bn, 1)
                dve.wait_ge(s_bn, s.n + 1)
                dve.bn_aggr(meanvar[:, ds(s.n, 1), :].rearrange("p o f -> p (o f)"), stats[:, s.slot(2), :]).then_inc(s_mv, 1)

            def deviation(s_std):
                dve.tensor_scalar(rstd[:, :], meanvar[:, :, 1], EPS, None, ALU.add).then_inc(s_std, 1)
                dve.wait_ge(s_std, 2)
                dve.reciprocal(rstd[:, :], rstd[:, :]).then_inc(s_std, 1)
                dve.wait_ge(s_std, 3)

            def layer0_rows(s):
                static = isinstance(s.n, int)
                if static and s.n == 0:
                    stage_block(s, s_stage, s_conv)
                if not (static and s.n == NB - 1):
                    stage_block(s + 1, s_stage, s_conv)
                dve.wait_ge(s_conv, s.n + 1)
                row = nodes[:, ds(s.n, 1), :].rearrange("p o f -> p (o f)")
                dve.scalar_tensor_tensor(out=row, in0=bank[s.slot(2)][:, 0:D], scalar=dinv[:, ds(s.n, 1)], in1=row,
                                         op0=ALU.mult, op1=ALU.add).then_inc(s_row, 1)
                statistics(s, s_row, s_bn, s_mv)

            dve.wait_ge(s_pre, v_xb)
            for n in range(NB):
                layer0_rows(Step(n))
            pre_wait(v_xb)
            v_off = pre(dve.memset(off[:, :], 0.0))
            v_acc = pre(dve.memset(acc[:, :], 0.0))
            dve.wait_ge(s_mv, NB)
            deviation(s_rstd)

            def normalise(s):
                if not (isinstance(s.n, int) and s.n < 2):
                    dve.wait_ge(s_tr, (s - 2).n + 1)
                row = nodes[:, ds(s.n, 1), :].rearrange("p o f -> p (o f)")
                mean, r = meanvar[:, ds(s.n, 1), 0], rstd[:, ds(s.n, 1)]
                dve.tensor_scalar(stage[:, s.slot(2), :], row, mean, r, ALU.subtract, ALU.mult).then_inc(s_norm, 1)
                dve.tensor_scalar(row, row, mean, r, ALU.subtract, ALU.mult)

            run_steps(dve, NB, 3, 2, 2, normalise)

            def split_lo(s):
                dve.wait_ge(s_hi, s.tick + 1)
                dve.tensor_tensor(xsplit[RAD:P, s.slot(2), :, :], xraw[RAD:P, s.slot(4), :, :],
                                  xsplit[RAD:P, s.slot(2), :, :].bitcast(F32), ALU.subtract).then_inc(s_lo, 1)

            def one_hot_t(s):
                b = s.slot(2)
                dve.wait_ge(s_rr[s.slot(4) // 2], s.round(4) * 16 + 16)
                if not (isinstance(s.n, int) and s.n < 2):
                    dve.wait_ge(s_q, (s - 2).tick + 1)
                dve.tensor_scalar(onehot_t[:, b, :], relrow_sb[:, s.slot(4), :], iota_part[0:WIN, :], None,
                                  ALU.is_equal).then_inc(s_hott, 1)

            def step2(s):
                static = isinstance(s.n, int)
                b, k = s.slot(2), s.slot(4)
                if static and s.n == 0:
                    split_lo(s)
                    split_lo(s + 1)
                    one_hot_t(s)
                if not (static and s.n >= G - 1):
                    one_hot_t(s + 1)
                if not (static and s.n < 2):
                    dve.wait_ge(s_sum2, (s - 2).tick + 1)
                one_hot(s)
                kv = gath[:, k, :].rearrange("p (t c f) -> p t c f", t=TILES, c=2)
                dve.wait_ge(s_gath2[k], s.round(4) * 16 * TILES + 16 * TILES)
                dve.wait_ge(s_q, s.tick + 1)
                dve.tensor_tensor(prod[:, :, :], kv[:, :, 0, :], q_ps[:, :].rearrange("p (t f) -> p t f", t=TILES),
                                  ALU.mult).then_inc(s_qk, 1)
                if not (static and s.n == 0):
                    add_window(s - 1, sum_ps, s_sum2, s_acc2, static and s.n == 1)
                dve.wait_ge(s_w, s.tick + 1)
                dve.wait_ge(s_qk, s.tick + 1)
                flat = prod[:, :, :].rearrange("p t f -> p (t f)")
                dve.tensor_tensor(flat, flat, w_ps[b][:, :], ALU.mult).then_inc(s_qkw, 1)
                if not (static and s.n >= G - 2):
                    split_lo(s + 2)
                dve.wait_ge(s_qkw, s.tick + 1)
                dve.tensor_reduce(red[:, :], flat.rearrange("p (h d) -> p h d", d=HD), AX.X, ALU.add).then_inc(s_red, 1)
                dve.wait_ge(s_red, s.tick + 1)
                weight = cut[:, ds(s.n * TILES, TILES)].unsqueeze(2).to_broadcast([P, TILES, HEADS])
                dve.tensor_tensor(alpha[:, :].rearrange("p (t h) -> p t h", h=HEADS),
                                  red[:, :].rearrange("p (t h) -> p t h", h=HEADS), weight, ALU.mult).then_inc(s_al, 1)
                dve.wait_ge(s_al, s.tick + 1)
                a = alpha[:, :].rearrange("p (t h) -> p t h", h=HEADS).unsqueeze(3).to_broadcast([P, TILES, HEADS, HD])
                dve.tensor_tensor(msg[:, b, :, :].rearrange("p t (h d) -> p t h d", d=HD),
                                  kv[:, :, 1, :].rearrange("p t (h d) -> p t h d", d=HD), a, ALU.mult).then_inc(s_msg, 1)
                if static and s.n == G - 1:
                    add_window(s, sum_ps, s_sum2, s_acc2, False)

            pre_wait(v_acc)
            with dve.Fori(0, n_pass) as p:
                start_pass(p, s_pass2, True)
                run_steps(dve, G, FIRST, UNROLL, LAST, step2, p)
                dve.wait_ge(s_acc2, p * G + G)

            def layer1_rows(s):
                static = isinstance(s.n, int)
                if static and s.n == 0:
                    stage_block(s, s_fstage, s_ftr)
                if not (static and s.n == NB - 1):
                    stage_block(s + 1, s_fstage, s_ftr)
                dve.wait_ge(s_ftr, s.n + 1)
                row = nodes[:, ds(s.n, 1), :].rearrange("p o f -> p (o f)")
                dve.tensor_tensor(row, row, bank[s.slot(2)][:, 0:D], ALU.add).then_inc(s_frow, 1)
                statistics(s, s_frow, s_fbn, s_fmv)

            for n in range(NB):
                layer1_rows(Step(n))
            dve.wait_ge(s_fmv, NB)
            deviation(s_frstd)
            dve.tensor_tensor(nodes[:, :, :], nodes[:, :, :],
                              meanvar[:, :, 0:1].to_broadcast([P, NB, D]), ALU.subtract).then_inc(s_fnorm, 1)
            dve.wait_ge(s_fnorm, 1)
            dve.tensor_tensor(nodes[:, :, :], nodes[:, :, :],
                              rstd[:, :].unsqueeze(2).to_broadcast([P, NB, D]), ALU.mult).then_inc(s_fnorm, 1)


class PRE:
    viol = 8
    passes = 10
    b1 = 26
    deg = 29
    xs = 32


def _pad(a, n, fill):
    import numpy as np
    out = np.full((n,) + a.shape[1:], fill, a.dtype)
    out[:a.shape[0]] = a
    return out


def kernel(**inputs):
    import numpy as np
    import concourse.bacc as bacc
    from concourse.bass_utils import run_bass_kernel_spmd

    a = {k: np.asarray(v) for k, v in inputs.items()}
    n, e = a["x"].shape[0], a["src"].shape[0]
    groups = -(-e // GE)
    groups += groups % 2
    ep, nb = groups * GE, -(-n // P)
    src, dst = _pad(a["src"], ep, n), _pad(a["dst"], ep, n)
    cut = _pad(a["edge_weight"], ep, 0)

    def columns(v):
        return np.ascontiguousarray(v.reshape(-1, P).T)

    arrays = {
        "x": a["x"],
        "x_pad": np.ascontiguousarray(_pad(a["x"], nb * P, 0).reshape(nb, P, -1).transpose(1, 0, 2)),
        "src_idx": columns(src).reshape(P, groups, TILES),
        "src_e": columns(src),
        "dst_e": columns(dst),
        "dst_row": dst.reshape(groups, GE),
        "dst_first": np.ascontiguousarray(dst.reshape(groups, GE)[:, 0]).reshape(1, groups),
        "cut_e": columns(cut),
        "rad_t": np.ascontiguousarray(_pad(a["edge_attr_64"], ep, 0).T),
        "sph_t": np.ascontiguousarray(_pad(a["edge_attr_32"], ep, 0).T),
        "w_l0": a["L0_gnn_weight"], "b_l0": a["L0_gnn_bias"],
        "wq": a["L1_gnn_wq"], "wk": a["L1_gnn_wk"], "wv": a["L1_gnn_wv"],
    }
    for m in ("rad", "sph"):
        for w in ("w0", "b0", "w1", "b1"):
            arrays[f"{m}_{w}"] = a[f"L1_gnn_{m}_{w}"]

    nc = bacc.Bacc("TRN2", target_bir_lowering=False, num_devices=1)
    args = {k: nc.dram_tensor(f"in_{k}", v.shape, mybir.dt.from_np(v.dtype), kind="ExternalInput").ap()
            for k, v in arrays.items()}
    args["out"] = nc.dram_tensor("out_0", a["x"].shape, F32, kind="ExternalOutput").ap()
    build(nc, **args)
    r = run_bass_kernel_spmd(nc, [{f"in_{k}": v for k, v in arrays.items()}], core_ids=[0])
    return r.results[0]["out_0"]
```

```python
from contextlib import ExitStack

import concourse.bass as bass
from concourse import mybir

P = 128
WIN = 64
TILES = 4
GE = P * TILES
HEADS, HD = 8, 16
RAD, SPH, HID = 64, 32, 256
EPS = 1e-5
AVG_NEIGHBORS = 16.0
UNROLL = 4
FIRST, LAST = 3, 2

F32 = mybir.dt.float32
F32R = mybir.dt.float32r
BF16 = mybir.dt.bfloat16
I32 = mybir.dt.int32
ALU = mybir.AluOpType
ACT = mybir.ActivationFunctionType
AX = mybir.AxisListType


class Step:

    def __init__(self, c, unroll=1, i=0, p=0, total=0):
        self.c, self.unroll, self.i, self.p, self.total = c, unroll, i, p, total

    @property
    def n(self):
        return self.i * self.unroll + self.c

    @property
    def tick(self):
        return self.p * self.total + self.n

    def before(self, k):
        return isinstance(self.n, int) and self.n < k

    def is_last(self, k=1):
        return isinstance(self.n, int) and self.n >= self.total - k

    def slot(self, k):
        return self.c % k

    def round(self, k):
        per_pass = (self.total - self.slot(k) + k - 1) // k
        return self.p * per_pass + self.i * (self.unroll // k) + self.c // k

    def __add__(self, d):
        return Step(self.c + d, self.unroll, self.i, self.p, self.total)

    def __sub__(self, d):
        return self + (-d)


class MlpSemaphores:
    def __init__(self, sem, sems, w):
        self.s_x = sems(f"s_x_{w}_", 2)
        self.s_hi = sem(f"s_hi_{w}")
        self.s_lo = sem(f"s_lo_{w}")
        self.s_l1 = sem(f"s_l1_{w}")
        self.s_silu = sem(f"s_silu_{w}")
        self.s_w = sem(f"s_w_{w}")


def run_steps(eng, total, step, p=0):
    turns = (total - FIRST - LAST) // UNROLL
    assert FIRST + turns * UNROLL + LAST == total and turns > 0
    for c in range(FIRST):
        step(Step(c, p=p, total=total))
    with eng.Fori(0, turns) as i:
        for j in range(UNROLL):
            step(Step(FIRST + j, UNROLL, i, p, total))
    for c in range(total - LAST, total):
        step(Step(c, p=p, total=total))


def at(eng, value):
    return value if isinstance(value, int) else eng.snap(value)


def ds(start, size):
    return bass.DynSlice(start, size)


def build(nc, x, x_pad, src_idx, src_e, dst_e, dst_row, dst_first, cut_e, rad_t, sph_t, w_l0, b_l0, rad_w0, rad_b0,
          rad_w1, rad_b1, sph_w0, sph_b0, sph_w1, sph_b1, wq, wk, wv, out):
    N, D = x.shape
    NB = x_pad.shape[1]
    NP = NB * P
    G = dst_row.shape[0]
    COLS = G * TILES
    WINDOWS = NP // WIN
    PAIRS = G // 2
    assert NP <= WIN * WINDOWS and N + WIN <= NP + WIN - 1
    DEG_COLS = 8
    DEG_STEPS = COLS // DEG_COLS
    HI = NP // WIN

    with ExitStack() as ctx:
        def sb(name, shape, dt=F32):
            return ctx.enter_context(nc.sbuf_tensor(name, shape, dt))

        def sem(name):
            return ctx.enter_context(nc.semaphore(name))

        def sems(name, k):
            return [sem(f"{name}{i}") for i in range(k)]

        first_d = nc.dram_tensor("first_d", (1, PAIRS), F32).ap()
        relrow_d = nc.dram_tensor("relrow_d", (G, GE), BF16).ap()
        xs_d = nc.dram_tensor("xs_d", (NP, D), F32).ap()
        kv_d = nc.dram_tensor("kv_d", (NP, 2 * D), F32).ap()
        w_d = nc.dram_tensor("w_d", (PAIRS * P, TILES * D), F32).ap()
        q_d = nc.dram_tensor("q_d", (NP + WIN, D), F32).ap()

        acc = sb("acc", [P, NP + WIN])
        nodes = sb("nodes", [P, NB, D])
        gath = sb("gath", [P, 4, TILES * 2 * D])
        idx = sb("idx", [P, 4, 2 * TILES], I32)
        onehot = sb("onehot", [P, 2, 2 * TILES, WIN])
        onehot_t = sb("onehot_t", [WIN, 2, GE])
        relrow_sb = sb("relrow_sb", [WIN, 4, GE], BF16)
        qwin = sb("qwin", [WIN, 2, D])
        xraw = sb("xraw", [P, 2, 2, GE])
        xsplit = sb("xsplit", [P, 2, 2, GE], F32R)
        hid = sb("hid", [P, 2, 4, GE])
        prod = sb("prod", [P, 2, TILES * D])
        w_sb = sb("w_sb", [P, 2, TILES * D])
        msg = sb("msg", [P, 2, TILES, D])
        red = sb("red", [P, 2, TILES, HEADS])
        alpha = sb("alpha", [P, 2, TILES, HEADS])
        rel0 = sb("rel0", [P, COLS])
        rel = sb("rel", [P, COLS])
        cut = sb("cut", [P, COLS])
        relrow0 = sb("relrow0", [PAIRS, 2, GE])
        relrow = sb("relrow", [PAIRS, 2, GE], BF16)
        base_f = sb("base_f", [P, PAIRS])
        base_i = sb("base_i", [1, PAIRS], I32)
        off = sb("off", [P, 1])
        passes_i = sb("passes_i", [1, 1], I32)
        iota_win = sb("iota_win", [P, WIN])
        iota_part = sb("iota_part", [P, 1])
        ident = sb("ident", [P, P])
        ones = sb("ones", [P, P])
        ones_bf = sb("ones_bf", [3, P], BF16)
        small = sb("small", [P, 16])
        dinv = sb("dinv", [P, NB])
        deg = sb("deg", [P, NB])
        w_l0_sb = sb("w_l0_sb", [P, D])
        b_l0_sb = sb("b_l0_sb", [P, D])
        wqkv = sb("wqkv", [P, 3 * D])
        w0_raw = sb("w0_raw", [P, 2, HID])
        w0_hi = sb("w0_hi", [P, 2, HID], F32R)
        w0_lo = sb("w0_lo", [P, 2, HID], F32R)
        b0 = sb("b0", [P, 4])
        w1 = sb("w1", [P, 4, D])
        b1_row = sb("b1_row", [1, 3, D])
        b1_parts = sb("b1_parts", [1, 3, TILES * D], BF16)
        b1_bf = sb("b1_bf", [3, TILES * D], BF16)
        stage = sb("stage", [P, 2, P])
        x_t = sb("x_t", [P, 2, P])
        qkv = sb("qkv", [P, 2, 3 * D])
        stats = sb("stats", [P, 2, 6])
        meanvar = sb("meanvar", [P, NB, 2])
        rstd = sb("rstd", [P, NB])
        src_i = sb("src_i", [P, COLS], I32)
        dig_i = sb("dig_i", [P, 2, COLS], I32)
        dig = sb("dig", [P, 2, COLS], BF16)
        iota_dig = sb("iota_dig", [P, WIN, DEG_COLS], BF16)
        iota_tmp = sb("iota_tmp", [P, WIN, DEG_COLS])
        lo_hot = sb("lo_hot", [P, 2, WIN, DEG_COLS], BF16)
        hi_hot = sb("hi_hot", [P, 2, HI, DEG_COLS], BF16)
        dst_ei = src_i
        dst_rowi = sb("dst_rowi", [PAIRS, 2, GE], I32)
        dst_f = sb("dst_f", [P, COLS])

        xs_sb = gath[:, :, :].rearrange("p a b -> p (a b)")[:, 0:NB * D].rearrange("p (b f) -> p b f", b=NB)

        bank = [ctx.enter_context(nc.psum_tensor(f"bank{i}", [P, 512], F32)) for i in range(8)]
        hid_ps = bank[0:4]
        w_ps = bank[4]
        q_ps = bank[5:7]
        sum_ps = bank[7]
        sum1_ps = bank[5:7]

        s_dst = sem("s_dst")
        s_src = sem("s_src")
        s_wts = sem("s_wts")
        s_const = sem("s_const")
        s_first = sem("s_first")
        s_firstb = sem("s_firstb")
        s_pre = sem("s_pre")
        s_viol = sem("s_viol")
        s_hot = sem("s_hot")
        s_degmm = sem("s_degmm")
        s_degp = sem("s_degp")
        s_xs = sem("s_xs")
        s_b1 = sem("s_b1")
        s_wsplit = sem("s_wsplit")
        s_pass1 = sem("s_pass1")
        s_idx1 = sems("s_idx1_", 4)
        s_gath1 = sems("s_gath1_", 4)
        s_hot1 = sem("s_hot1")
        s_sum1 = sem("s_sum1")
        s_acc1 = sem("s_acc1")
        s_stage = sem("s_stage")
        s_conv = sem("s_conv")
        s_row = sem("s_row")
        s_bn = sem("s_bn")
        s_mv = sem("s_mv")
        s_rstd = sem("s_rstd")
        s_norm = sem("s_norm")
        s_tr = sem("s_tr")
        s_trc = sem("s_trc")
        s_proj = sem("s_proj")
        s_projc = sem("s_projc")
        s_table = sems("s_table", 2)
        s_go = sem("s_go")
        s_sp_pass = sem("s_sp_pass")
        s_pass2 = sem("s_pass2")
        s_relrow = sem("s_relrow")
        s_idx2 = sems("s_idx2_", 4)
        s_gath2 = sems("s_gath2_", 4)
        s_rr = sems("s_rr", 2)
        s_qw = sems("s_qw", 2)
        mlp1, mlp2 = MlpSemaphores(sem, sems, 1), MlpSemaphores(sem, sems, 2)
        s_wcopy = sem("s_wcopy")
        s_wstore = sems("s_wstore", 2)
        s_wload = sems("s_wload", 2)
        s_hott = sem("s_hott")
        s_q = sem("s_q")
        s_qk = sem("s_qk")
        s_qkw = sem("s_qkw")
        s_red = sem("s_red")
        s_al = sem("s_al")
        s_msg = sem("s_msg")
        s_sum2 = sem("s_sum2")
        s_acc2 = sem("s_acc2")
        s_fstage = sem("s_fstage")
        s_ftr = sem("s_ftr")
        s_frow = sem("s_frow")
        s_fbn = sem("s_fbn")
        s_fmv = sem("s_fmv")
        s_frstd = sem("s_frstd")
        s_fnorm = sem("s_fnorm")
        s_out = sem("s_out")

        WEIGHTS = 16 * 19
        TABLES = [32 * ((NB + 1) // 2) + 16, 32 * (NB // 2)]
        block = ctx.enter_context(nc.Block())

        def passes(eng):
            return eng.value_load(passes_i[0:1, 0:1], min_val=1, max_val=WINDOWS)


        @block.sync
        def _(sp):
            sp.dma_start(base_i[:, :], dst_first).then_inc(s_dst, 16)
            sp.dma_start(dst_ei[:, :], dst_e).then_inc(s_dst, 16)
            sp.dma_start(dst_rowi[:, :, :], dst_row.rearrange("(p j) e -> p j e", j=2)).then_inc(s_dst, 16)
            sp.dma_start(nodes[:, :, :], x_pad).then_inc(s_wts, 16)
            sp.dma_start(cut[:, :], cut_e).then_inc(s_wts, 16)
            sp.dma_start(w_l0_sb[:, :], w_l0).then_inc(s_wts, 16)
            sp.dma_start(b_l0_sb[:, :], b_l0.partition_broadcast(P)).then_inc(s_wts, 16)
            for j, w in enumerate((wq, wk, wv)):
                sp.dma_start(wqkv[:, j * D:(j + 1) * D], w).then_inc(s_wts, 16)
            for j in range(2):
                sp.dma_start(w0_raw[j * RAD:(j + 1) * RAD, 0, :], rad_w0).then_inc(s_wts, 16)
            for j in range(4):
                sp.dma_start(w0_raw[j * SPH:(j + 1) * SPH, 1, :], sph_w0).then_inc(s_wts, 16)
            for j, b in enumerate((rad_b0, sph_b0)):
                sp.dma_start(b0[:, 2 * j:2 * j + 2], b.rearrange("(c p) -> p c", p=P),
                             allow_slow_non_contiguous=True).then_inc(s_wts, 16)
            for j, w in enumerate((rad_w1, sph_w1)):
                sp.dma_start(w1[:, 2 * j:2 * j + 2, :], w.rearrange("(c p) f -> p c f", p=P)).then_inc(s_wts, 16)
            for j, b in enumerate((rad_b1, sph_b1)):
                sp.dma_start(b1_row[0:1, j, :], b.rearrange("(o f) -> o f", o=1)).then_inc(s_wts, 16)
            sp.wait_ge(s_pre, 1)
            sp.dma_start(first_d, base_f[0:1, :]).then_inc(s_first, 16)
            sp.wait_ge(s_first, 16)
            sp.dma_start(base_f[:, :], first_d[0, :].partition_broadcast(P)).then_inc(s_firstb, 16)
            sp.wait_ge(s_pre, 2)
            sp.dma_start(src_i[:, :], src_e).then_inc(s_src, 16)
            sp.wait_ge(s_pre, PRE.b1)
            sp.dma_start(b1_bf[:, :], b1_parts[0:1, :, :]).then_inc(s_b1, 16)
            sp.wait_ge(s_pre, PRE.xs)
            sp.dma_start(xs_d.rearrange("(b p) f -> p b f", p=P), xs_sb).then_inc(s_xs, 16)

            n_pass = passes(sp)

            def load_features(s, mlp, odd):
                edge = at(sp, (s.n * 2 + odd) * GE)
                if not s.before(2):
                    sp.wait_ge(mlp.s_lo, (s - 2).tick + 1)
                for j in range(2):
                    sp.dma_start(xraw[j * RAD:(j + 1) * RAD, s.slot(2), 0, :],
                                 rad_t[:, ds(edge, GE)]).then_inc(mlp.s_x[s.slot(2)], 16)
                for j in range(4):
                    sp.dma_start(xraw[j * SPH:(j + 1) * SPH, s.slot(2), 1, :],
                                 sph_t[:, ds(edge, GE)]).then_inc(mlp.s_x[s.slot(2)], 16)

            def load_idx(s, s_idx, s_gath):
                first = at(sp, s.n * 2)
                if not s.before(4):
                    for j in range(2):
                        sp.wait_ge(s_gath[2 * s.slot(2) + j], ((s - 4).round(2) + 1) * 16 * TILES)
                sp.dma_start(idx[:, s.slot(4), :].rearrange("p (j t) -> p j t", j=2),
                             src_idx[:, ds(first, 2), :]).then_inc(s_idx[s.slot(4)], 16)

            def store_weights(s):
                row = at(sp, s.n * P)
                sp.wait_ge(s_wcopy, s.tick + 1)
                sp.dma_start(w_d[ds(row, P), :],
                             w_sb[:, s.slot(2), :]).then_inc(s_wstore[s.slot(2)], 16)

            def sweep1(s):
                load_idx(s, s_idx1, s_gath1)
                load_features(s, mlp1, 0)
                if not s.before(3):
                    store_weights(s - 3)
                if s.is_last():
                    store_weights(s - 2)
                    store_weights(s - 1)
                    store_weights(s)

            with sp.Fori(0, n_pass) as p:
                run_steps(sp, PAIRS, sweep1, p)
                sp.wait_ge(s_acc1, p * PAIRS + PAIRS)
                sp.sem_inc(s_sp_pass, 1)
                for j in range(2):
                    sp.wait_ge(s_wstore[j], (p + 1) * 16 * ((PAIRS + 1 - j) // 2))
                    sp.sem_inc(s_sp_pass, 1)

            def store_tables(s):
                node = at(sp, s.n * P)
                sp.wait_ge(s_projc, s.n + 1)
                sp.dma_start(kv_d[ds(node, P), :], qkv[:, s.slot(2), D:3 * D]).then_inc(s_table[s.slot(2)], 16)
                sp.dma_start(q_d[ds(node, P), :], qkv[:, s.slot(2), 0:D]).then_inc(s_table[s.slot(2)], 16)

            run_steps(sp, NB, store_tables)
            sp.dma_start(q_d[NP:NP + WIN, :], qkv[0:WIN, 0, 0:D]).then_inc(s_table[0], 16)
            for j in range(2):
                sp.wait_ge(s_table[j], TABLES[j])

            def sweep2(s):
                a, h = s.slot(2), slice(2 * s.slot(2), 2 * s.slot(2) + 2)
                load_idx(s, s_idx2, s_gath2)
                load_features(s, mlp2, 1)
                row, first = at(sp, s.n * P), at(sp, s.n * 2)
                if not s.before(2):
                    sp.wait_ge(s_hott, (s - 2).tick * 2 + 2)
                sp.dma_start(relrow_sb[:, h, :],
                             relrow_d[ds(first, 2), :].partition_broadcast(WIN)).then_inc(s_rr[a], 16)
                base = sp.value_load(base_i[0:1, ds(s.n, 1)], min_val=0, max_val=NP - 1)
                if not s.before(2):
                    sp.wait_ge(s_q, (s - 2).tick * 2 + 2)
                sp.dma_start(qwin[:, a, :], q_d[ds(base, WIN), :]).then_inc(s_qw[a], 16)
                if not s.before(2):
                    sp.wait_ge(s_qkw, (s - 2).tick * 2 + 1)
                sp.dma_start(w_sb[:, a, :],
                             w_d[ds(row, P), :]).then_inc(s_wload[a], 16)

            with sp.Fori(0, n_pass) as p:
                sp.wait_ge(s_pass2, p * 4 + 3)
                sp.dma_start(relrow_d.rearrange("(p j) e -> p j e", j=2), relrow[:, :, :]).then_inc(s_relrow, 16)
                sp.wait_ge(s_relrow, p * 16 + 16)
                run_steps(sp, PAIRS, sweep2, p)
                sp.wait_ge(s_acc2, p * PAIRS + PAIRS)
                sp.sem_inc(s_sp_pass, 1)

            full = N // P
            sp.wait_ge(s_fnorm, 2)
            sp.dma_start(out[0:full * P, :].rearrange("(b p) f -> p b f", p=P), nodes[:, 0:full, :]).then_inc(s_out, 16)
            sp.dma_start(out[full * P:N, :], nodes[0:N - full * P, full, :]).then_inc(s_out, 16)
            sp.wait_ge(s_out, 32)
            sp.wait_ge(s_xs, 16)

        @block.gpsimd
        def _(pool):
            pool.iota(iota_tmp[:, :, :], [[1, WIN], [0, DEG_COLS]], base=0, channel_multiplier=0,
                      allow_small_or_imprecise_dtypes=True).then_inc(s_const, 1)
            pool.iota(iota_win[:, :], [[1, WIN]], base=0, channel_multiplier=0,
                      allow_small_or_imprecise_dtypes=True).then_inc(s_const, 1)
            pool.iota(iota_part[:, :], [[0, 1]], base=0, channel_multiplier=1,
                      allow_small_or_imprecise_dtypes=True).then_inc(s_const, 1)
            pool.memset(ones[:, :], 1.0).then_inc(s_const, 1)
            pool.memset(ones_bf[:, :], 1.0).then_inc(s_const, 1)
            pool.memset(acc[:, :], 0.0).then_inc(s_const, 1)
            pool.memset(ident[:, :], 0.0).then_inc(s_const, 1)
            pool.wait_ge(s_const, 7)
            pool.affine_select(out=ident[:, :], in_=ident[:, :], compare_op=ALU.not_equal, fill=1.0, base=0,
                               pattern=[[-1, P]], channel_multiplier=1).then_inc(s_const, 1)
            pool.wait_ge(s_pre, PRE.passes)
            n_pass = passes(pool)
            pool.wait_ge(s_xs, 16)

            def gather(s, s_idx, s_gath, used, table, width):
                pool.wait_ge(s_idx[s.slot(4)], s.round(4) * 16 + 16)
                for j in range(2):
                    k = 2 * s.slot(2) + j
                    if not s.before(2):
                        pool.wait_ge(*used(s - 2, j))
                    pool.sem_inc(s_go, 1)
                    for t in range(TILES):
                        pool.indirect_dma_start(gath[:, k, t * width:(t + 1) * width], None, table,
                                                bass.IndirectOffsetOnAxis(ap=idx[:, s.slot(4), j * TILES + t:j * TILES + t + 1], axis=0)
                                                ).then_inc(s_gath[k], 16)

            def used1(s, j):
                return s_sum1, s.tick + 1

            def used2(s, j):
                return s_msg, s.tick * 2 + j + 1

            with pool.Fori(0, n_pass) as p:
                run_steps(pool, PAIRS, lambda s: gather(s, s_idx1, s_gath1, used1, xs_d, D), p)
                pool.wait_ge(s_acc1, p * PAIRS + PAIRS)

            for j in range(2):
                pool.wait_ge(s_table[j], TABLES[j])

            with pool.Fori(0, n_pass) as p:
                run_steps(pool, PAIRS, lambda s: gather(s, s_idx2, s_gath2, used2, kv_d, 2 * D), p)
                pool.wait_ge(s_acc2, p * PAIRS + PAIRS)

        @block.scalar
        def _(act):
            act.wait_ge(s_pre, PRE.passes)
            n_pass = passes(act)
            act.wait_ge(s_pre, PRE.deg)
            act.activation(dinv[:, :], dinv[:, :], ACT.Sqrt).then_inc(s_degp, 1)
            act.wait_ge(s_wts, WEIGHTS)

            def split_hi(s, mlp):
                act.wait_ge(mlp.s_x[s.slot(2)], (s.round(2) + 1) * 96)
                if not s.before(2):
                    act.wait_ge(mlp.s_l1, ((s - 2).tick + 1) * 4)
                act.activation(xsplit[:, s.slot(2), :, :], xraw[:, s.slot(2), :, :], ACT.Copy).then_inc(mlp.s_hi, 1)

            def silu(s, mlp):
                for c in range(4):
                    act.wait_ge(mlp.s_l1, s.tick * 4 + c + 1)
                    if c == 0 and not s.before(2):
                        act.wait_ge(mlp.s_w, (s - 2).tick + 1)
                    act.activation(hid[:, s.slot(2), c, :], hid_ps[c][:, :], ACT.Silu,
                                   bias=b0[:, c:c + 1]).then_inc(mlp.s_silu, 1)

            def activate(s, mlp):
                if s.before(1):
                    split_hi(s, mlp)
                    split_hi(s + 1, mlp)
                    silu(s, mlp)
                if not s.is_last(2):
                    split_hi(s + 2, mlp)
                if not s.is_last():
                    silu(s + 1, mlp)

            def sweep1(s):
                activate(s, mlp1)
                act.wait_ge(mlp1.s_w, s.tick + 1)
                if not s.before(2):
                    act.wait_ge(s_wstore[s.slot(2)], ((s - 2).round(2) + 1) * 16)
                act.activation(w_sb[:, s.slot(2), :], w_ps[:, :], ACT.Copy).then_inc(s_wcopy, 1)

            with act.Fori(0, n_pass) as p:
                run_steps(act, PAIRS, sweep1, p)
                for j in range(2):
                    act.wait_ge(s_wstore[j], (p + 1) * 16 * ((PAIRS + 1 - j) // 2))
                act.wait_ge(s_acc1, p * PAIRS + PAIRS)

            act.wait_ge(s_rstd, 1)
            act.activation(rstd[:, :], rstd[:, :], ACT.Sqrt).then_inc(s_rstd, 1)

            def copy_projection(s):
                b = s.slot(2)
                act.wait_ge(s_proj, s.n + 1)
                if not s.before(2):
                    act.wait_ge(s_table[b], (s - 2).round(2) * 32 + 32)
                act.mul(qkv[:, b, 0:D], bank[4 + b][:, 0:D], 1.0 / (HD ** 0.5 * AVG_NEIGHBORS))
                act.activation(qkv[:, b, D:3 * D], bank[4 + b][:, D:3 * D], ACT.Copy).then_inc(s_projc, 1)

            def evacuate(s):
                b = s.slot(2)
                act.wait_ge(s_tr, s.n + 1)
                if not s.before(2):
                    act.wait_ge(s_proj, (s - 2).n + 1)
                act.activation(x_t[:, b, :], bank[2 + b][:, 0:P], ACT.Copy).then_inc(s_trc, 1)
                if not s.before(1):
                    copy_projection(s - 1)
                if s.is_last():
                    copy_projection(s)

            run_steps(act, NB, evacuate)

            with act.Fori(0, n_pass) as p:
                run_steps(act, PAIRS, lambda s: activate(s, mlp2), p)
                act.wait_ge(s_acc2, p * PAIRS + PAIRS)
            act.wait_ge(s_frstd, 1)
            act.activation(rstd[:, :], rstd[:, :], ACT.Sqrt).then_inc(s_frstd, 1)

        @block.tensor
        def _(pe):
            pe.wait_ge(s_const, 8)
            pe.wait_ge(s_pre, PRE.viol)
            pe.matmul(bank[0][:, 0:1], ones[:, :], small[:, 2:3], start=True, stop=True).then_inc(s_viol, 1)

            def count(s):
                b = s.slot(2)
                pe.wait_ge(s_hot, s.n + 1)
                for t in range(DEG_COLS):
                    one = isinstance(s.n, int)
                    mm = pe.matmul(bank[1][0:WIN, 0:HI], lo_hot[:, b, :, t], hi_hot[:, b, :, t],
                                   start=(one and s.n == 0 and t == 0),
                                   stop=(one and s.n == DEG_STEPS - 1 and t == DEG_COLS - 1),
                                   skip_group_check=True)
                mm.then_inc(s_degmm, 1)

            run_steps(pe, DEG_STEPS, count)
            n_pass = passes(pe)

            pe.wait_ge(s_wts, WEIGHTS)
            pe.wait_ge(s_wsplit, 4)
            pe.wait_ge(s_b1, 16)

            def layer1(s, mlp):
                b = s.slot(2)
                pe.wait_ge(mlp.s_lo, s.tick + 1)
                for c in range(4):
                    if not s.before(1):
                        pe.wait_ge(mlp.s_silu, (s - 1).tick * 4 + c + 1)
                    m, cols = c // 2, slice((c % 2) * P, (c % 2) * P + P)
                    mm = pe.matmul(hid_ps[c][:, :], w0_hi[:, m, cols], xsplit[:, b, m, :], start=True, stop=(m == 1))
                    if m == 0:
                        mm = pe.matmul(hid_ps[c][:, :], w0_lo[:, m, cols], xsplit[:, b, m, :], start=False, stop=True)
                    mm.then_inc(mlp.s_l1, 1)

            def layer2(s, mlp, s_read, per_step):
                b = s.slot(2)
                if not s.before(1):
                    pe.wait_ge(s_read, s.tick * per_step)
                pe.matmul(w_ps[:, :], ones_bf[:, :], b1_bf[:, :], start=True, stop=False, skip_group_check=True)
                for c in range(4):
                    pe.wait_ge(mlp.s_silu, s.tick * 4 + c + 1)
                    for t in range(TILES):
                        mm = pe.matmul(w_ps[:, t * D:(t + 1) * D], hid[:, b, c, t * P:(t + 1) * P], w1[:, c, :],
                                       start=False, stop=(c == 3), skip_group_check=True)
                mm.then_inc(mlp.s_w, 1)

            def sum1(s):
                b = s.slot(2)
                pe.wait_ge(s_hot1, s.tick + 1)
                if not s.before(2):
                    pe.wait_ge(s_acc1, (s - 2).tick + 1)
                for j in range(2):
                    k = 2 * b + j
                    pe.wait_ge(s_gath1[k], (s.round(2) + 1) * 16 * TILES)
                    for t in range(TILES):
                        mm = pe.matmul(sum1_ps[b][:, 0:WIN], gath[:, k, t * D:(t + 1) * D],
                                       onehot[:, b, j * TILES + t, :], start=(j == 0 and t == 0),
                                       stop=(j == 1 and t == TILES - 1))
                mm.then_inc(s_sum1, 1)

            def sweep1(s):
                if s.before(1):
                    layer1(s, mlp1)
                if not s.is_last():
                    layer1(s + 1, mlp1)
                sum1(s)
                layer2(s, mlp1, s_wcopy, 1)

            with pe.Fori(0, n_pass) as p:
                run_steps(pe, PAIRS, sweep1, p)
                pe.wait_ge(s_acc1, p * PAIRS + PAIRS)
                pe.wait_ge(s_wcopy, p * PAIRS + PAIRS)


            def convolve(s):
                b = s.slot(2)
                pe.wait_ge(s_stage, s.n + 1)
                if not s.before(2):
                    pe.wait_ge(s_row, (s - 2).n + 1)
                pe.matmul(bank[b][:, 0:D], stage[:, b, :], w_l0_sb[:, :], start=True, stop=True).then_inc(s_conv, 1)

            run_steps(pe, NB, convolve)

            def project(s):
                b = s.slot(2)
                pe.wait_ge(s_trc, s.n + 1)
                if not s.before(2):
                    pe.wait_ge(s_projc, (s - 2).n + 1)
                pe.matmul(bank[4 + b][:, 0:3 * D], x_t[:, b, :], wqkv[:, :], start=True, stop=True).then_inc(s_proj, 1)

            def transpose_project(s):
                b = s.slot(2)
                pe.wait_ge(s_norm, s.n + 1)
                if not s.before(2):
                    pe.wait_ge(s_trc, (s - 2).n + 1)
                pe.transpose(bank[2 + b][:, 0:P], stage[:, b, :], ident[:, :]).then_inc(s_tr, 1)
                if not s.before(1):
                    project(s - 1)

            run_steps(pe, NB, transpose_project)
            project(Step(NB - 1))
            pe.wait_ge(s_projc, NB)

            def expand_q(s, j):
                pe.wait_ge(s_hott, s.tick * 2 + j + 1)
                if j == 0:
                    pe.wait_ge(s_qw[s.slot(2)], (s.round(2) + 1) * 16)
                if not s.before(1):
                    pe.wait_ge(s_qk, (s - 1).tick * 2 + j + 1)
                for t in range(TILES):
                    mm = pe.matmul(q_ps[j][:, t * D:(t + 1) * D], onehot_t[:, j, t * P:(t + 1) * P],
                                   qwin[:, s.slot(2), :], start=True, stop=True, skip_group_check=True)
                mm.then_inc(s_q, 1)

            def sum2(s, j):
                pe.wait_ge(s_msg, s.tick * 2 + j + 1)
                if j == 0 and not s.before(1):
                    pe.wait_ge(s_acc2, s.tick)
                for t in range(TILES):
                    mm = pe.matmul(sum_ps[:, 0:WIN], msg[:, j, t, :], onehot[:, s.slot(2), j * TILES + t, :],
                                   start=(j == 0 and t == 0), stop=(j == 1 and t == TILES - 1),
                                   skip_group_check=True)
                mm.then_inc(s_sum2, 1)

            def sweep2(s):
                if s.before(1):
                    layer1(s, mlp2)
                    expand_q(s, 0)
                    expand_q(s, 1)
                if not s.is_last():
                    layer1(s + 1, mlp2)
                if not s.before(1):
                    sum2(s - 1, 1)
                layer2(s, mlp2, s_qkw, 2)
                if not s.is_last():
                    expand_q(s + 1, 0)
                sum2(s, 0)
                if not s.is_last():
                    expand_q(s + 1, 1)
                else:
                    sum2(s, 1)

            with pe.Fori(0, n_pass) as p:
                run_steps(pe, PAIRS, sweep2, p)
                pe.wait_ge(s_acc2, p * PAIRS + PAIRS)

            def transpose_back(s):
                b = s.slot(2)
                pe.wait_ge(s_fstage, s.n + 1)
                if not s.before(2):
                    pe.wait_ge(s_frow, (s - 2).n + 1)
                pe.transpose(bank[b][:, 0:P], stage[:, b, :], ident[:, :]).then_inc(s_ftr, 1)

            run_steps(pe, NB, transpose_back)

        @block.vector
        def _(dve):
            done = [0]

            def pre(ins):
                done[0] += 1
                ins.then_inc(s_pre, 1)
                return done[0]

            def pre_wait(v):
                dve.wait_ge(s_pre, v)

            def pair_bcast(row):
                return row.unsqueeze(2).to_broadcast([P, PAIRS, 2 * TILES])

            def by_pair(t):
                return t.rearrange("p (g t) -> p g t", t=2 * TILES)

            dve.wait_ge(s_dst, 48)
            pre(dve.tensor_copy(base_f[0:1, :], base_i[:, :]))
            v_dst = pre(dve.tensor_copy(dst_f[:, :], dst_ei[:, :]))
            v_row = pre(dve.tensor_copy(relrow0[:, :, :], dst_rowi[:, :, :]))
            dve.wait_ge(s_firstb, 16)
            pre_wait(v_dst)
            v = pre(dve.tensor_tensor(by_pair(rel[:, :]), by_pair(dst_f[:, :]), pair_bcast(base_f[:, :]), ALU.subtract))
            pre_wait(v)
            pre(dve.tensor_reduce(small[:, 0:1], rel[:, :], AX.X, ALU.max))
            v = pre(dve.tensor_reduce(small[:, 1:2], rel[:, :], AX.X, ALU.min))
            pre_wait(v)
            v = pre(dve.tensor_scalar(small[:, 0:1], small[:, 0:1], WIN - 0.5, None, ALU.is_gt))
            pre_wait(v)
            v = pre(dve.scalar_tensor_tensor(out=small[:, 2:3], in0=small[:, 1:2], scalar=-0.5, in1=small[:, 0:1],
                                             op0=ALU.is_lt, op1=ALU.add))
            assert v == PRE.viol, v
            dve.wait_ge(s_viol, 1)
            v = pre(dve.tensor_scalar(small[:, 3:4], bank[0][:, 0:1], 0.5, None, ALU.is_lt))
            pre_wait(v)
            v = pre(dve.tensor_scalar(passes_i[:, :], small[0:1, 3:4], float(1 - WINDOWS), float(WINDOWS),
                                      ALU.mult, ALU.add))
            assert v == PRE.passes, v
            v = pre(dve.tensor_scalar(base_f[:, :], base_f[:, :], small[:, 3:4], None, ALU.mult))
            v_rb = pre(dve.tensor_scalar(small[0:PAIRS, 4:5], relrow0[:, 0, 0:1], small[0:PAIRS, 3:4], None, ALU.mult))
            pre_wait(v)
            pre(dve.tensor_tensor(by_pair(rel0[:, :]), by_pair(dst_f[:, :]), pair_bcast(base_f[:, :]), ALU.subtract))
            pre_wait(v_rb)
            pre(dve.tensor_scalar(relrow0[:, :, :], relrow0[:, :, :], small[0:PAIRS, 4:5], None, ALU.subtract))

            dve.wait_ge(s_const, 8)
            pre(dve.tensor_copy(iota_dig[:, :, :], iota_tmp[:, :, :]))
            dve.wait_ge(s_src, 16)
            pre(dve.tensor_scalar(dig_i[:, 0, :], src_i[:, :], WIN - 1, None, ALU.bitwise_and))
            v = pre(dve.tensor_scalar(dig_i[:, 1, :], src_i[:, :], WIN.bit_length() - 1, None, ALU.logical_shift_right))
            pre_wait(v)
            v = pre(dve.tensor_copy(dig[:, :, :], dig_i[:, :, :]))
            pre_wait(v)

            def hots(s):
                b = s.slot(2)
                if not s.before(2):
                    dve.wait_ge(s_degmm, (s - 2).n + 1)
                for j, (hot, w) in enumerate(((lo_hot, WIN), (hi_hot, HI))):
                    digits = dig[:, j, ds(s.n * DEG_COLS, DEG_COLS)].unsqueeze(1).to_broadcast([P, w, DEG_COLS])
                    last = dve.tensor_tensor(hot[:, b, :, :], digits, iota_dig[:, 0:w, :], ALU.is_equal)
                last.then_inc(s_hot, 1)

            run_steps(dve, DEG_STEPS, hots)

            dve.wait_ge(s_wts, WEIGHTS)
            dve.tensor_copy(w0_hi[:, :, :], w0_raw[:, :, :]).then_inc(s_wsplit, 1)
            dve.wait_ge(s_wsplit, 1)
            dve.tensor_tensor(w0_lo[:, :, :], w0_raw[:, :, :], w0_hi[:, :, :].bitcast(F32), ALU.subtract).then_inc(s_wsplit, 1)
            dve.wait_ge(s_wsplit, 2)
            for j in (1, 3):
                dve.tensor_tensor(w0_hi[j * SPH:(j + 1) * SPH, 1, :], w0_raw[j * SPH:(j + 1) * SPH, 1, :],
                                  w0_hi[j * SPH:(j + 1) * SPH, 1, :].bitcast(F32), ALU.subtract).then_inc(s_wsplit, 1)
            v = pre(dve.tensor_tensor(b1_row[:, 2, :], b1_row[:, 0, :], b1_row[:, 1, :], ALU.add))
            for part in range(3):
                pre_wait(v)
                v = pre(dve.tensor_copy(b1_parts[:, part, :].rearrange("p (t f) -> p t f", t=TILES),
                                        b1_row[:, 2:3, :].to_broadcast([1, TILES, D])))
                if part < 2:
                    pre_wait(v)
                    v = pre(dve.tensor_tensor(b1_row[:, 2, :], b1_row[:, 2, :], b1_parts[:, part, 0:D], ALU.subtract))
            assert v == PRE.b1, v

            dve.wait_ge(s_degmm, DEG_STEPS)
            by_half = bank[1][0:WIN, 0:HI].rearrange("p (b h) -> p h b", h=2)
            pre(dve.tensor_copy(deg[0:WIN, :], by_half[:, 0, :]))
            v = pre(dve.tensor_copy(deg[WIN:P, :], by_half[:, 1, :]))
            pre_wait(v)
            v = pre(dve.tensor_scalar(dinv[:, :], deg[:, :], 1.0, None, ALU.max))
            assert v == PRE.deg, v
            dve.wait_ge(s_degp, 1)
            v = pre(dve.reciprocal(dinv[:, :], dinv[:, :]))
            pre_wait(v)
            v = pre(dve.scalar_tensor_tensor(out=dinv[:, :], in0=deg[:, :], scalar=0.5, in1=dinv[:, :],
                                             op0=ALU.is_gt, op1=ALU.mult))
            pre_wait(v)
            v = pre(dve.tensor_tensor(xs_sb, nodes[:, :, :], dinv[:, :].unsqueeze(2).to_broadcast([P, NB, D]), ALU.mult))
            assert v == PRE.xs, v
            pre_wait(v)
            v_xb = pre(dve.tensor_tensor(nodes[:, :, :], nodes[:, :, :],
                                         b_l0_sb[:, :].unsqueeze(1).to_broadcast([P, NB, D]), ALU.add))

            v = pre(dve.memset(off[:, :], 0.0))
            pre_wait(v)
            n_pass = passes(dve)

            def start_pass(p, s_pass, rows):
                dve.tensor_scalar(rel[:, :], rel0[:, :], off[:, 0:1], None, ALU.subtract).then_inc(s_pass, 1)
                if rows:
                    dve.tensor_scalar(relrow[:, :, :], relrow0[:, :, :], off[0:PAIRS, 0:1], None,
                                      ALU.subtract).then_inc(s_pass, 1)
                else:
                    dve.tensor_copy(small[:, 6:7], off[:, 0:1]).then_inc(s_pass, 1)
                dve.tensor_scalar(base_i[:, :], base_f[0:1, :], off[0:1, 0:1], None, ALU.add).then_inc(s_pass, 1)
                dve.wait_ge(s_pass, p * 4 + 3)
                dve.tensor_scalar(off[:, :], off[:, :], float(WIN), None, ALU.add).then_inc(s_pass, 1)
                dve.wait_ge(s_pass, p * 4 + 4)

            def one_hot(s):
                at = rel[:, ds(s.n * 2 * TILES, 2 * TILES)].unsqueeze(2).to_broadcast([P, 2 * TILES, WIN])
                nodes_in = iota_win[:, :].unsqueeze(1).to_broadcast([P, 2 * TILES, WIN])
                return dve.tensor_tensor(onehot[:, s.slot(2), :, :], at, nodes_in, ALU.is_equal)

            def split_lo(s, mlp):
                dve.wait_ge(mlp.s_hi, s.tick + 1)
                dve.tensor_tensor(xsplit[RAD:P, s.slot(2), :, :], xraw[RAD:P, s.slot(2), :, :],
                                  xsplit[RAD:P, s.slot(2), :, :].bitcast(F32), ALU.subtract).then_inc(mlp.s_lo, 1)

            bases = [None] * UNROLL

            def load_base(s):
                if isinstance(s.n, int):
                    bases[0] = dve.value_load(base_i[0:1, s.n - 1:s.n], min_val=0, max_val=NP - 1)
                elif s.c == FIRST:
                    _, bases[:] = nc.values_load_multi_w_load_instructions(
                        base_i[0:1, ds(s.n - 1, UNROLL)], engines=[mybir.EngineType.DVE], min_val=0, max_val=NP - 1,
                        skip_runtime_bounds_check_because="base_i holds node numbers")
                else:
                    bases.append(bases.pop(0))

            def add_window(s, ps, value, s_sum, s_acc):
                dve.wait_ge(s_sum, value)
                if not s.before(1):
                    dve.wait_ge(s_acc, s.tick)
                here = acc[:, ds(bases[0], WIN)]
                dve.tensor_tensor(here, here, ps[:, 0:WIN], ALU.add).then_inc(s_acc, 1)

            def sweep1(s):
                if not s.before(1):
                    load_base(s)
                if s.before(1):
                    one_hot(s).then_inc(s_hot1, 1)
                    split_lo(s, mlp1)
                    split_lo(s + 1, mlp1)
                if not s.is_last():
                    if not s.before(1):
                        dve.wait_ge(s_sum1, s.tick)
                    one_hot(s + 1).then_inc(s_hot1, 1)
                if not s.before(1):
                    add_window(s - 1, sum1_ps[(s - 1).slot(2)], s.tick, s_sum1, s_acc1)
                if not s.is_last(2):
                    split_lo(s + 2, mlp1)
                if s.is_last():
                    load_base(s + 1)
                    add_window(s, sum1_ps[s.slot(2)], s.tick + 1, s_sum1, s_acc1)

            with dve.Fori(0, n_pass) as p:
                start_pass(p, s_pass1, False)
                run_steps(dve, PAIRS, sweep1, p)
                dve.wait_ge(s_acc1, p * PAIRS + PAIRS)

            def stage_block(s, s_stage, s_used):
                if not s.before(2):
                    dve.wait_ge(s_used, (s - 2).n + 1)
                dve.tensor_copy(stage[:, s.slot(2), :], acc[:, ds(s.n * P, P)]).then_inc(s_stage, 1)

            def statistics(s, s_row, s_bn, s_mv):
                dve.wait_ge(s_row, s.n + 1)
                dve.bn_stats(stats[:, s.slot(2), :], nodes[:, ds(s.n, 1), :].rearrange("p o f -> p (o f)")).then_inc(s_bn, 1)
                dve.wait_ge(s_bn, s.n + 1)
                dve.bn_aggr(meanvar[:, ds(s.n, 1), :].rearrange("p o f -> p (o f)"), stats[:, s.slot(2), :]).then_inc(s_mv, 1)

            def deviation(s_std):
                dve.tensor_scalar(rstd[:, :], meanvar[:, :, 1], EPS, None, ALU.add).then_inc(s_std, 1)
                dve.wait_ge(s_std, 2)
                dve.reciprocal(rstd[:, :], rstd[:, :]).then_inc(s_std, 1)
                dve.wait_ge(s_std, 3)

            def layer0_rows(s):
                static = isinstance(s.n, int)
                if static and s.n == 0:
                    stage_block(s, s_stage, s_conv)
                if not static or s.n < NB - 1:
                    stage_block(s + 1, s_stage, s_conv)
                dve.wait_ge(s_conv, s.n + 1)
                row = nodes[:, ds(s.n, 1), :].rearrange("p o f -> p (o f)")
                dve.scalar_tensor_tensor(out=row, in0=bank[s.slot(2)][:, 0:D], scalar=dinv[:, ds(s.n, 1)], in1=row,
                                         op0=ALU.mult, op1=ALU.add).then_inc(s_row, 1)
                statistics(s, s_row, s_bn, s_mv)

            dve.wait_ge(s_pre, v_xb)
            for n in range(NB):
                layer0_rows(Step(n))
            pre_wait(v_xb)
            v_off = pre(dve.memset(off[:, :], 0.0))
            v_acc = pre(dve.memset(acc[:, :], 0.0))
            dve.wait_ge(s_mv, NB)
            deviation(s_rstd)

            def normalise(s):
                if not s.before(2):
                    dve.wait_ge(s_tr, (s - 2).n + 1)
                row = nodes[:, ds(s.n, 1), :].rearrange("p o f -> p (o f)")
                mean, r = meanvar[:, ds(s.n, 1), 0], rstd[:, ds(s.n, 1)]
                dve.tensor_scalar(stage[:, s.slot(2), :], row, mean, r, ALU.subtract, ALU.mult).then_inc(s_norm, 1)
                dve.tensor_scalar(row, row, mean, r, ALU.subtract, ALU.mult)

            run_steps(dve, NB, normalise)

            def one_hot_t(s, j):
                dve.wait_ge(s_rr[s.slot(2)], (s.round(2) + 1) * 16)
                if not s.before(1):
                    dve.wait_ge(s_q, (s - 1).tick * 2 + j + 1)
                dve.tensor_scalar(onehot_t[:, j, :], relrow_sb[:, 2 * s.slot(2) + j, :], iota_part[0:WIN, :], None,
                                  ALU.is_equal).then_inc(s_hott, 1)

            def sweep2(s):
                kv = [gath[:, 2 * s.slot(2) + j, :].rearrange("p (t c f) -> p t c f", t=TILES, c=2) for j in range(2)]

                def times_k(j):
                    dve.wait_ge(s_gath2[2 * s.slot(2) + j], (s.round(2) + 1) * 16 * TILES)
                    dve.wait_ge(s_q, s.tick * 2 + j + 1)
                    dve.tensor_tensor(prod[:, j, :].rearrange("p (t f) -> p t f", t=TILES), kv[j][:, :, 0, :],
                                      q_ps[j][:, :].rearrange("p (t f) -> p t f", t=TILES), ALU.mult).then_inc(s_qk, 1)

                def times_w(j):
                    dve.wait_ge(s_qk, s.tick * 2 + j + 1)
                    if j == 0:
                        dve.wait_ge(s_wload[s.slot(2)], (s.round(2) + 1) * 16)
                        w = w_sb[:, s.slot(2), :]
                    else:
                        dve.wait_ge(mlp2.s_w, s.tick + 1)
                        w = w_ps[:, :]
                    dve.tensor_tensor(prod[:, j, :], prod[:, j, :], w, ALU.mult).then_inc(s_qkw, 1)

                def head_sums(j):
                    dve.wait_ge(s_qkw, s.tick * 2 + j + 1)
                    dve.tensor_reduce(red[:, j, :, :].rearrange("p t h -> p (t h)"),
                                      prod[:, j, :].rearrange("p (h d) -> p h d", d=HD), AX.X, ALU.add).then_inc(s_red, 1)

                def times_cutoff(j):
                    weight = cut[:, ds(s.n * 2 * TILES + j * TILES, TILES)].unsqueeze(2).to_broadcast([P, TILES, HEADS])
                    dve.wait_ge(s_red, s.tick * 2 + j + 1)
                    dve.tensor_tensor(alpha[:, j, :, :], red[:, j, :, :], weight, ALU.mult).then_inc(s_al, 1)

                def message(j):
                    a = alpha[:, j, :, :].unsqueeze(3).to_broadcast([P, TILES, HEADS, HD])
                    dve.wait_ge(s_al, s.tick * 2 + j + 1)
                    dve.tensor_tensor(msg[:, j, :, :].rearrange("p t (h d) -> p t h d", d=HD),
                                      kv[j][:, :, 1, :].rearrange("p t (h d) -> p t h d", d=HD), a,
                                      ALU.mult).then_inc(s_msg, 1)

                if s.before(1):
                    split_lo(s, mlp2)
                    split_lo(s + 1, mlp2)
                    one_hot(s)
                    one_hot_t(s, 0)
                    one_hot_t(s, 1)
                else:
                    load_base(s)
                times_k(0)
                times_k(1)
                times_w(0)
                if not s.before(1):
                    add_window(s - 1, sum_ps, s.tick * 2, s_sum2, s_acc2)
                head_sums(0)
                if not s.is_last():
                    one_hot_t(s + 1, 0)
                times_cutoff(0)
                if not s.is_last():
                    one_hot_t(s + 1, 1)
                message(0)
                if not s.is_last(2):
                    split_lo(s + 2, mlp2)
                times_w(1)
                if not s.is_last():
                    one_hot(s + 1)
                head_sums(1)
                times_cutoff(1)
                message(1)
                if s.is_last():
                    load_base(s + 1)
                    add_window(s, sum_ps, s.tick * 2 + 2, s_sum2, s_acc2)

            pre_wait(v_acc)
            with dve.Fori(0, n_pass) as p:
                start_pass(p, s_pass2, True)
                run_steps(dve, PAIRS, sweep2, p)
                dve.wait_ge(s_acc2, p * PAIRS + PAIRS)

            def layer1_rows(s):
                static = isinstance(s.n, int)
                if static and s.n == 0:
                    stage_block(s, s_fstage, s_ftr)
                if not static or s.n < NB - 1:
                    stage_block(s + 1, s_fstage, s_ftr)
                dve.wait_ge(s_ftr, s.n + 1)
                row = nodes[:, ds(s.n, 1), :].rearrange("p o f -> p (o f)")
                dve.tensor_tensor(row, row, bank[s.slot(2)][:, 0:D], ALU.add).then_inc(s_frow, 1)
                statistics(s, s_frow, s_fbn, s_fmv)

            for n in range(NB):
                layer1_rows(Step(n))
            dve.wait_ge(s_fmv, NB)
            deviation(s_frstd)
            dve.tensor_tensor(nodes[:, :, :], nodes[:, :, :],
                              meanvar[:, :, 0:1].to_broadcast([P, NB, D]), ALU.subtract).then_inc(s_fnorm, 1)
            dve.wait_ge(s_fnorm, 1)
            dve.tensor_tensor(nodes[:, :, :], nodes[:, :, :],
                              rstd[:, :].unsqueeze(2).to_broadcast([P, NB, D]), ALU.mult).then_inc(s_fnorm, 1)


class PRE:
    viol = 8
    passes = 10
    b1 = 24
    deg = 27
    xs = 30


def _pad(a, n, fill):
    import numpy as np
    out = np.full((n,) + a.shape[1:], fill, a.dtype)
    out[:a.shape[0]] = a
    return out


def kernel(**inputs):
    import numpy as np
    import concourse.bacc as bacc
    from concourse.bass_utils import run_bass_kernel_spmd

    a = {k: np.asarray(v) for k, v in inputs.items()}
    n, e = a["x"].shape[0], a["src"].shape[0]
    groups = -(-e // GE)
    groups += groups % 2
    ep, nb = groups * GE, -(-n // P)
    src, dst = _pad(a["src"], ep, n), _pad(a["dst"], ep, n)
    cut = _pad(a["edge_weight"], ep, 0)

    def columns(v):
        return np.ascontiguousarray(v.reshape(-1, P).T)

    arrays = {
        "x": a["x"],
        "x_pad": np.ascontiguousarray(_pad(a["x"], nb * P, 0).reshape(nb, P, -1).transpose(1, 0, 2)),
        "src_idx": columns(src).reshape(P, groups, TILES),
        "src_e": columns(src),
        "dst_e": columns(dst),
        "dst_row": dst.reshape(groups, GE),
        "dst_first": np.ascontiguousarray(dst.reshape(-1, 2 * GE)[:, 0]).reshape(1, -1),
        "cut_e": columns(cut),
        "rad_t": np.ascontiguousarray(_pad(a["edge_attr_64"], ep, 0).T),
        "sph_t": np.ascontiguousarray(_pad(a["edge_attr_32"], ep, 0).T),
        "w_l0": a["L0_gnn_weight"], "b_l0": a["L0_gnn_bias"],
        "wq": a["L1_gnn_wq"], "wk": a["L1_gnn_wk"], "wv": a["L1_gnn_wv"],
    }
    for m in ("rad", "sph"):
        for w in ("w0", "b0", "w1", "b1"):
            arrays[f"{m}_{w}"] = a[f"L1_gnn_{m}_{w}"]

    nc = bacc.Bacc("TRN2", target_bir_lowering=False, num_devices=1)
    args = {k: nc.dram_tensor(f"in_{k}", v.shape, mybir.dt.from_np(v.dtype), kind="ExternalInput").ap()
            for k, v in arrays.items()}
    args["out"] = nc.dram_tensor("out_0", a["x"].shape, F32, kind="ExternalOutput").ap()
    build(nc, **args)
    r = run_bass_kernel_spmd(nc, [{f"in_{k}": v for k, v in arrays.items()}], core_ids=[0])
    return r.results[0]["out_0"]
```

```python
from contextlib import ExitStack

import concourse.bass as bass
from concourse import mybir

P = 128
WIN = 64
TILES = 4
GE = P * TILES
HEADS, HD = 8, 16
RAD, SPH, HID = 64, 32, 256
EPS = 1e-5
AVG_NEIGHBORS = 16.0
UNROLL = 4
FIRST, LAST = 3, 2
CHUNK = 4

F32 = mybir.dt.float32
F32R = mybir.dt.float32r
BF16 = mybir.dt.bfloat16
I32 = mybir.dt.int32
ALU = mybir.AluOpType
ACT = mybir.ActivationFunctionType
AX = mybir.AxisListType


class Step:

    def __init__(self, c, unroll=1, i=0, p=0, total=0):
        self.c, self.unroll, self.i, self.p, self.total = c, unroll, i, p, total

    @property
    def n(self):
        return self.i * self.unroll + self.c

    @property
    def tick(self):
        return self.p * self.total + self.n

    def before(self, k):
        return isinstance(self.n, int) and self.n < k

    def is_last(self, k=1):
        return isinstance(self.n, int) and self.n >= self.total - k

    def slot(self, k):
        return self.c % k

    def round(self, k):
        per_pass = (self.total - self.slot(k) + k - 1) // k
        return self.p * per_pass + self.i * (self.unroll // k) + self.c // k

    def __add__(self, d):
        return Step(self.c + d, self.unroll, self.i, self.p, self.total)

    def __sub__(self, d):
        return self + (-d)


class MlpSemaphores:
    def __init__(self, sem, sems, w):
        self.s_x = sems(f"s_x_{w}_", 2)
        self.s_hi = sem(f"s_hi_{w}")
        self.s_lo = sem(f"s_lo_{w}")
        self.s_l1 = sem(f"s_l1_{w}")
        self.s_silu = sem(f"s_silu_{w}")
        self.s_w = sem(f"s_w_{w}")


def run_steps(eng, total, step, p=0):
    turns = (total - FIRST - LAST) // UNROLL
    assert FIRST + turns * UNROLL + LAST == total and turns > 0
    for c in range(FIRST):
        step(Step(c, p=p, total=total))
    with eng.Fori(0, turns) as i:
        for j in range(UNROLL):
            step(Step(FIRST + j, UNROLL, i, p, total))
    for c in range(total - LAST, total):
        step(Step(c, p=p, total=total))


def at(eng, value):
    return value if isinstance(value, int) else eng.snap(value)


def ds(start, size):
    return bass.DynSlice(start, size)


def build(nc, x, x_pad, src_idx, src_e, dst_e, dst_row, dst_first, cut_e, rad_t, sph_t, w_l0, b_l0, rad_w0, rad_b0,
          rad_w1, rad_b1, sph_w0, sph_b0, sph_w1, sph_b1, wq, wk, wv, out):
    N, D = x.shape
    NB = x_pad.shape[1]
    NP = NB * P
    G = dst_row.shape[0]
    COLS = G * TILES
    WINDOWS = NP // WIN
    PAIRS = G // 2
    DEG_COLS = 18
    DEG_STEPS = -(-COLS // DEG_COLS)
    DEG_STEPS += (FIRST + LAST - DEG_STEPS) % UNROLL
    CHUNKS = -(-NB // CHUNK)
    XS_DVE = 0, NB * 3 // 10, NB * 6 // 10
    XS_ACT = NB * 6 // 10, NB * 8 // 10, NB
    HI = NP // WIN

    with ExitStack() as ctx:
        def sb(name, shape, dt=F32):
            return ctx.enter_context(nc.sbuf_tensor(name, shape, dt))

        def sem(name):
            return ctx.enter_context(nc.semaphore(name))

        def sems(name, k):
            return [sem(f"{name}{i}") for i in range(k)]

        first_d = nc.dram_tensor("first_d", (1, PAIRS), F32).ap()
        relrow_d = nc.dram_tensor("relrow_d", (G, GE), BF16).ap()
        xs_d = nc.dram_tensor("xs_d", (NP, D), F32).ap()
        kv_d = nc.dram_tensor("kv_d", (NP, 2 * D), F32).ap()
        w_d = nc.dram_tensor("w_d", (PAIRS * P, TILES * D), F32).ap()
        q_d = nc.dram_tensor("q_d", (3, NP + WIN, D), BF16).ap()

        acc = sb("acc", [P, NP + WIN])
        nodes = sb("nodes", [P, NB, D])
        gath = sb("gath", [P, 4, TILES * 2 * D])
        idx = sb("idx", [P, 4, 2 * TILES], I32)
        onehot = sb("onehot", [P, 2, 2 * TILES, WIN])
        onehot_t = sb("onehot_t", [P, 2, GE], BF16)
        relrow_sb = sb("relrow_sb", [P, 4, GE], BF16)
        qwin = sb("qwin", [P, 2, 2, D], BF16)
        xraw = sb("xraw", [RAD, 2, 2, GE])
        xsplit = sb("xsplit", [P, 2, 2, GE], F32R)
        hid = sb("hid", [P, 2, 4, GE])
        prod = sb("prod", [P, 2, TILES * D])
        w_sb = sb("w_sb", [P, 2, TILES * D])
        msg = sb("msg", [P, 2, TILES, D])
        red = sb("red", [P, 2, TILES, HEADS])
        alpha = sb("alpha", [P, 2, TILES, HEADS])
        rel0 = sb("rel0", [P, COLS])
        rel = sb("rel", [P, COLS])
        cut = sb("cut", [P, COLS])
        relrow0 = sb("relrow0", [PAIRS, 2, GE])
        relrow = sb("relrow", [PAIRS, 2, GE], BF16)
        base_f = sb("base_f", [P, PAIRS])
        base_i = sb("base_i", [1, PAIRS], I32)
        off = sb("off", [P, 1])
        passes_i = sb("passes_i", [1, 1], I32)
        iota_win = sb("iota_win", [P, WIN])
        iota_part = sb("iota_part", [P, 1])
        ident = sb("ident", [P, P])
        ones = sb("ones", [P, P])
        ones_bf = sb("ones_bf", [3, P], BF16)
        small = sb("small", [P, 16])
        dinv = sb("dinv", [P, NB])
        deg = sb("deg", [P, NB])
        w_l0_sb = sb("w_l0_sb", [P, D])
        b_l0_sb = sb("b_l0_sb", [P, D])
        wqkv = sb("wqkv", [P, 3 * D])
        w0_raw = sb("w0_raw", [P, 2, HID])
        w0_hi = sb("w0_hi", [P, 2, HID], F32R)
        w0_lo = sb("w0_lo", [P, 2, HID], F32R)
        b0 = sb("b0", [P, 4])
        w1 = sb("w1", [P, 4, D])
        b1_row = sb("b1_row", [1, 3, D])
        b1_parts = sb("b1_parts", [1, 3, TILES * D], BF16)
        b1_bf = sb("b1_bf", [3, TILES * D], BF16)
        x_t = sb("x_t", [P, 2, CHUNK * P])
        stats = sb("stats", [P, NB, 6])
        shift = sb("shift", [P, NB])
        q_parts = sb("q_parts", [P, 4, 3, CHUNK * D], BF16)
        q_rest = sb("q_rest", [P, CHUNK * D])
        meanvar = sb("meanvar", [P, NB, 2])
        rstd = sb("rstd", [P, NB])
        src_i = sb("src_i", [P, COLS], I32)
        dig_i = sb("dig_i", [P, 2, COLS], I32)
        dig = sb("dig", [P, 2, DEG_STEPS * DEG_COLS], BF16)
        iota_dig = sb("iota_dig", [P, WIN, DEG_COLS], BF16)
        iota_tmp = sb("iota_tmp", [P, WIN, DEG_COLS])
        lo_hot = sb("lo_hot", [P, 4, WIN, DEG_COLS], BF16)
        hi_hot = sb("hi_hot", [P, 4, HI, DEG_COLS], BF16)
        dst_ei = sb("dst_ei", [P, COLS], I32)
        dst_rowi = sb("dst_rowi", [PAIRS, 2, GE], I32)
        dst_f = sb("dst_f", [P, COLS])

        xs_sb = gath[:, :, :].rearrange("p a b -> p (a b)")[:, 0:NB * D].rearrange("p (b f) -> p b f", b=NB)

        x_raw = hid[:, :, :, :].rearrange("p a b c -> p (a b c)")[:, 0:NB * D].rearrange("p (b f) -> p b f", b=NB)
        kv_out = gath[:, :, :].rearrange("p c (b f) -> p c b f", b=CHUNK)

        def blocks(c):
            return range(CHUNK * c, min(NB, CHUNK * (c + 1)))

        bank = [ctx.enter_context(nc.psum_tensor(f"bank{i}", [P, 512], F32)) for i in range(8)]
        hid_ps = bank[0:4]
        w_ps = bank[4]
        q_ps = bank[5:7]
        sum_ps = bank[7]
        sum1_ps = bank[5:7]

        s_dst = sem("s_dst")
        s_src = sem("s_src")
        s_wts = sem("s_wts")
        s_const = sem("s_const")
        s_first = sem("s_first")
        s_firstb = sem("s_firstb")
        s_pre = sem("s_pre")
        s_set = sem("s_set")
        s_viol = sem("s_viol")
        s_hot = sem("s_hot")
        s_degmm = sem("s_degmm")
        s_degp = sem("s_degp")
        s_xsa = sem("s_xsa")
        s_xs = sem("s_xs")
        s_b1 = sem("s_b1")
        s_pass1 = sem("s_pass1")
        s_idx1 = sems("s_idx1_", 4)
        s_gath1 = sems("s_gath1_", 4)
        s_hot1 = sem("s_hot1")
        s_sum1 = sem("s_sum1")
        s_acc1 = sem("s_acc1")
        s_conv = sem("s_conv")
        s_row = sem("s_row")
        s_bn = sem("s_bn")
        s_mv = sem("s_mv")
        s_var = sem("s_var")
        s_std = sem("s_std")
        s_inv = sem("s_inv")
        s_shift = sem("s_shift")
        s_norm = sem("s_norm")
        s_clear = sem("s_clear")
        s_tr = sem("s_tr")
        s_trc = sem("s_trc")
        s_projq = sem("s_projq")
        s_hi = sem("s_hi")
        s_rest = sem("s_rest")
        s_mid = sem("s_mid")
        s_lo = sem("s_lo")
        s_qt = sems("s_qt", 4)
        s_proj = sem("s_proj")
        s_projc = sem("s_projc")
        s_kvt = sems("s_kvt", 4)
        s_go = sem("s_go")
        s_sp_pass = sem("s_sp_pass")
        s_pass2 = sem("s_pass2")
        s_relrow = sem("s_relrow")
        s_idx2 = sems("s_idx2_", 4)
        s_gath2 = sems("s_gath2_", 4)
        s_rr = sems("s_rr", 2)
        s_qw = sems("s_qw", 2)
        mlp1, mlp2 = MlpSemaphores(sem, sems, 1), MlpSemaphores(sem, sems, 2)
        s_wcopy = sem("s_wcopy")
        s_wstore = sems("s_wstore", 2)
        s_wload = sems("s_wload", 2)
        s_hott = sem("s_hott")
        s_q = sem("s_q")
        s_qk = sem("s_qk")
        s_qkw = sem("s_qkw")
        s_red = sem("s_red")
        s_al = sem("s_al")
        s_msg = sem("s_msg")
        s_sum2 = sem("s_sum2")
        s_acc2 = sem("s_acc2")
        s_ftr = sem("s_ftr")
        s_frow = sem("s_frow")
        s_fbn = sem("s_fbn")
        s_fmv = sem("s_fmv")
        s_fvar = sem("s_fvar")
        s_fstd = sem("s_fstd")
        s_finv = sem("s_finv")
        s_fshift = sem("s_fshift")
        s_fnorm = sem("s_fnorm")
        s_out = sem("s_out")

        WEIGHTS = 16 * 19

        def chunks_in(slot, k):
            return len(range(slot, CHUNKS, k))

        block = ctx.enter_context(nc.Block())

        def passes(eng):
            return eng.value_load(passes_i[0:1, 0:1], min_val=1, max_val=WINDOWS)

        @block.sync
        def _(sp):
            sp.dma_start(src_i[:, :], src_e).then_inc(s_src, 16)
            sp.dma_start(base_i[:, :], dst_first).then_inc(s_dst, 16)
            sp.dma_start(dst_ei[:, :], dst_e).then_inc(s_dst, 16)
            sp.dma_start(dst_rowi[:, :, :], dst_row.rearrange("(p j) e -> p j e", j=2)).then_inc(s_dst, 16)
            sp.dma_start(x_raw, x_pad).then_inc(s_wts, 16)
            sp.dma_start(cut[:, :], cut_e).then_inc(s_wts, 16)
            sp.dma_start(w_l0_sb[:, :], w_l0).then_inc(s_wts, 16)
            sp.dma_start(b_l0_sb[:, :], b_l0.partition_broadcast(P)).then_inc(s_wts, 16)
            for j, w in enumerate((wq, wk, wv)):
                sp.dma_start(wqkv[:, j * D:(j + 1) * D], w).then_inc(s_wts, 16)
            for j in range(2):
                sp.dma_start(w0_raw[j * RAD:(j + 1) * RAD, 0, :], rad_w0).then_inc(s_wts, 16)
            for j in range(4):
                sp.dma_start(w0_raw[j * SPH:(j + 1) * SPH, 1, :], sph_w0).then_inc(s_wts, 16)
            for j, b in enumerate((rad_b0, sph_b0)):
                sp.dma_start(b0[:, 2 * j:2 * j + 2], b.rearrange("(c p) -> p c", p=P),
                             allow_slow_non_contiguous=True).then_inc(s_wts, 16)
            for j, w in enumerate((rad_w1, sph_w1)):
                sp.dma_start(w1[:, 2 * j:2 * j + 2, :], w.rearrange("(c p) f -> p c f", p=P)).then_inc(s_wts, 16)
            for j, b in enumerate((rad_b1, sph_b1)):
                sp.dma_start(b1_row[0:1, j, :], b.rearrange("(o f) -> o f", o=1)).then_inc(s_wts, 16)
            sp.wait_ge(s_set, SET.first)
            sp.dma_start(first_d, base_f[0:1, :]).then_inc(s_first, 16)
            sp.wait_ge(s_first, 16)
            sp.dma_start(base_f[:, :], first_d[0, :].partition_broadcast(P)).then_inc(s_firstb, 16)
            sp.wait_ge(s_set, SET.b1)
            sp.dma_start(b1_bf[:, :], b1_parts[0:1, :, :]).then_inc(s_b1, 16)
            xs_rows = xs_d.rearrange("(b p) f -> p b f", p=P)
            for j in range(2):
                sp.wait_ge(s_pre, PRE.xs + j)
                sp.dma_start(xs_rows[:, XS_DVE[j]:XS_DVE[j + 1], :],
                             xs_sb[:, XS_DVE[j]:XS_DVE[j + 1], :]).then_inc(s_xs, 16)
                sp.wait_ge(s_xsa, XS_ACT[j + 1] - XS_ACT[0])
                sp.dma_start(xs_rows[:, XS_ACT[j]:XS_ACT[j + 1], :],
                             xs_sb[:, XS_ACT[j]:XS_ACT[j + 1], :]).then_inc(s_xs, 16)

            sp.wait_ge(s_pre, PRE.passes)
            n_pass = passes(sp)

            def load_features(s, mlp, odd):
                edge = at(sp, (s.n * 2 + odd) * GE)
                if not s.before(2):
                    sp.wait_ge(mlp.s_lo, (s - 2).tick + 1)
                sp.dma_start(xraw[:, s.slot(2), 0, :], rad_t[:, ds(edge, GE)]).then_inc(mlp.s_x[s.slot(2)], 16)
                for j in range(2):
                    sp.dma_start(xraw[j * SPH:(j + 1) * SPH, s.slot(2), 1, :],
                                 sph_t[:, ds(edge, GE)]).then_inc(mlp.s_x[s.slot(2)], 16)

            def load_idx(s, s_idx, s_gath):
                first = at(sp, s.n * 2)
                if not s.before(4):
                    for j in range(2):
                        sp.wait_ge(s_gath[2 * s.slot(2) + j], ((s - 4).round(2) + 1) * 16 * TILES)
                sp.dma_start(idx[:, s.slot(4), :].rearrange("p (j t) -> p j t", j=2),
                             src_idx[:, ds(first, 2), :]).then_inc(s_idx[s.slot(4)], 16)

            def store_weights(s):
                row = at(sp, s.n * P)
                sp.wait_ge(s_wcopy, s.tick + 1)
                sp.dma_start(w_d[ds(row, P), :],
                             w_sb[:, s.slot(2), :]).then_inc(s_wstore[s.slot(2)], 16)

            def sweep1(s):
                load_idx(s, s_idx1, s_gath1)
                load_features(s, mlp1, 0)
                if not s.before(3):
                    store_weights(s - 3)
                if s.is_last():
                    store_weights(s - 2)
                    store_weights(s - 1)
                    store_weights(s)

            with sp.Fori(0, n_pass) as p:
                run_steps(sp, PAIRS, sweep1, p)
                sp.wait_ge(s_acc1, p * PAIRS + PAIRS)
                sp.sem_inc(s_sp_pass, 1)
                for j in range(2):
                    sp.wait_ge(s_wstore[j], (p + 1) * 16 * ((PAIRS + 1 - j) // 2))
                    sp.sem_inc(s_sp_pass, 1)

            for c in range(CHUNKS):
                n, rows = len(blocks(c)), slice(blocks(c)[0] * P, (blocks(c)[-1] + 1) * P)
                sp.wait_ge(s_projc, blocks(c)[-1] // 2 + 1)
                sp.dma_start(kv_d[rows, :].rearrange("(b p) f -> p b f", p=P),
                             kv_out[:, c % 4, 0:n, :]).then_inc(s_kvt[c % 4], 16)
                sp.wait_ge(s_lo, c + 1)
                for part in range(3):
                    sp.dma_start(q_d[part, rows, :].rearrange("(b p) f -> p b f", p=P),
                                 q_parts[:, c % 4, part, 0:n * D].rearrange("p (b f) -> p b f", f=D)
                                 ).then_inc(s_qt[c % 4], 16)
                    if c == 1:
                        sp.dma_start(q_d[part, NP:NP + WIN, :],
                                     q_parts[0:WIN, 1, part, 0:D]).then_inc(s_qt[1], 16)

            def sweep2(s):
                a, h = s.slot(2), slice(2 * s.slot(2), 2 * s.slot(2) + 2)
                load_idx(s, s_idx2, s_gath2)
                if s.before(1):
                    load_features(s, mlp2, 1)
                    load_features(s + 1, mlp2, 1)
                elif not s.before(2):
                    load_features(s, mlp2, 1)
                if s.before(1):
                    sp.wait_ge(s_pass2, s.p * 4 + 2)
                    sp.dma_start(relrow_d.rearrange("(p j) e -> p j e", j=2), relrow[:, :, :]).then_inc(s_relrow, 16)
                    sp.wait_ge(s_relrow, s.p * 16 + 16)
                row, first = at(sp, s.n * P), at(sp, s.n * 2)
                if not s.before(2):
                    sp.wait_ge(s_hott, (s - 2).tick * 2 + 2)
                sp.dma_start(relrow_sb[:, h, :],
                             relrow_d[ds(first, 2), :].partition_broadcast(P)).then_inc(s_rr[a], 16)
                base = sp.value_load(base_i[0:1, ds(s.n, 1)], min_val=0, max_val=NP - 1)
                if not s.before(2):
                    sp.wait_ge(s_q, (s - 2).tick * 2 + 2)
                if s.before(1):
                    for j in range(4):
                        sp.wait_ge(s_qt[j], 48 * (chunks_in(j, 4) + (j == 1)))
                for part, to in enumerate((qwin[0:WIN, a, 0, :], qwin[WIN:2 * WIN, a, 0, :], qwin[0:WIN, a, 1, :])):
                    sp.dma_start(to, q_d[part, ds(base, WIN), :]).then_inc(s_qw[a], 16)
                if not s.before(2):
                    sp.wait_ge(s_qkw, (s - 2).tick * 2 + 1)
                sp.dma_start(w_sb[:, a, :],
                             w_d[ds(row, P), :]).then_inc(s_wload[a], 16)

            with sp.Fori(0, n_pass) as p:
                run_steps(sp, PAIRS, sweep2, p)
                sp.wait_ge(s_acc2, p * PAIRS + PAIRS)
                sp.sem_inc(s_sp_pass, 1)

            for c in range(CHUNKS):
                sp.wait_ge(s_fnorm, blocks(c)[-1] + 1)
                full = [b for b in blocks(c) if (b + 1) * P <= N]
                if full:
                    sp.dma_start(out[full[0] * P:(full[-1] + 1) * P, :].rearrange("(b p) f -> p b f", p=P),
                                 nodes[:, full[0]:full[-1] + 1, :]).then_inc(s_out, 16)
            if N % P:
                sp.dma_start(out[N // P * P:N, :], nodes[0:N % P, N // P, :]).then_inc(s_out, 16)
            sp.wait_ge(s_out, 16 * (-(-(N // P) // CHUNK) + (1 if N % P else 0)))

        @block.gpsimd
        def _(pool):
            pool.iota(iota_tmp[:, :, :], [[1, WIN], [0, DEG_COLS]], base=0, channel_multiplier=0,
                      allow_small_or_imprecise_dtypes=True).then_inc(s_const, 1)
            pool.memset(dig[:, :, COLS:DEG_STEPS * DEG_COLS], 255.0).then_inc(s_const, 1)
            pool.iota(iota_win[:, :], [[1, WIN]], base=0, channel_multiplier=0,
                      allow_small_or_imprecise_dtypes=True).then_inc(s_const, 1)
            pool.wait_ge(s_const, 3)
            for j in range(P // WIN):
                pool.iota(iota_part[j * WIN:(j + 1) * WIN, :], [[0, 1]], base=0, channel_multiplier=1,
                          allow_small_or_imprecise_dtypes=True).then_inc(s_const, 1)
            pool.wait_ge(s_const, 5)
            pool.memset(ones[:, :], 1.0).then_inc(s_const, 1)
            pool.memset(ones_bf[:, :], 1.0).then_inc(s_const, 1)
            pool.memset(ident[:, :], 0.0).then_inc(s_const, 1)
            pool.wait_ge(s_const, 8)
            pool.affine_select(out=ident[:, :], in_=ident[:, :], compare_op=ALU.not_equal, fill=1.0, base=0,
                               pattern=[[-1, P]], channel_multiplier=1).then_inc(s_const, 1)
            pool.memset(acc[:, :], 0.0).then_inc(s_const, 1)

            done = [0]

            def step(ins):
                done[0] += 1
                ins.then_inc(s_set, 1)
                return done[0]

            def step_wait(v):
                pool.wait_ge(s_set, v)

            pool.wait_ge(s_dst, 48)
            v = step(pool.tensor_copy(base_f[0:1, :], base_i[:, :]))
            assert v == SET.first, v
            step_wait(v)
            v = step(pool.tensor_copy(dst_f[:, :], dst_ei[:, :]))
            step_wait(v)
            v = step(pool.tensor_copy(relrow0[:, :, :], dst_rowi[:, :, :]))
            step_wait(v)
            pool.wait_ge(s_firstb, 16)
            v = step(pool.tensor_tensor(rel[:, :].rearrange("p (g t) -> p g t", t=2 * TILES),
                                        dst_f[:, :].rearrange("p (g t) -> p g t", t=2 * TILES),
                                        base_f[:, :].unsqueeze(2).to_broadcast([P, PAIRS, 2 * TILES]), ALU.subtract))
            assert v == SET.rel, v

            pool.wait_ge(s_wts, WEIGHTS)
            step_wait(v)
            v = step(pool.tensor_tensor(b1_row[:, 2, :], b1_row[:, 0, :], b1_row[:, 1, :], ALU.add))
            for part in range(3):
                step_wait(v)
                v = step(pool.tensor_copy(b1_parts[:, part, :].rearrange("p (t f) -> p t f", t=TILES),
                                          b1_row[:, 2:3, :].to_broadcast([1, TILES, D])))
                if part < 2:
                    step_wait(v)
                    v = step(pool.tensor_tensor(b1_row[:, 2, :], b1_row[:, 2, :], b1_parts[:, part, 0:D], ALU.subtract))
            assert v == SET.b1, v
            step_wait(v)
            v = step(pool.tensor_copy(w0_hi[:, :, :], w0_raw[:, :, :]))
            step_wait(v)
            v = step(pool.tensor_tensor(w0_lo[:, :, :], w0_raw[:, :, :], w0_hi[:, :, :].bitcast(F32), ALU.subtract))
            step_wait(v)
            for j in (1, 3):
                v = step(pool.tensor_tensor(w0_hi[j * SPH:(j + 1) * SPH, 1, :], w0_raw[j * SPH:(j + 1) * SPH, 1, :],
                                            w0_hi[j * SPH:(j + 1) * SPH, 1, :].bitcast(F32), ALU.subtract))
                step_wait(v)
            step(pool.tensor_scalar(wqkv[:, 0:D], wqkv[:, 0:D], 1.0 / (HD ** 0.5 * AVG_NEIGHBORS), None, ALU.mult))
            v = step(pool.tensor_tensor(nodes[:, :, :], x_raw, b_l0_sb[:, :].unsqueeze(1).to_broadcast([P, NB, D]),
                                        ALU.add))
            assert v == SET.all, v

            pool.wait_ge(s_pre, PRE.passes)
            n_pass = passes(pool)
            pool.wait_ge(s_xs, 64)

            def gather(s, s_idx, s_gath, used, table, width):
                rows = idx[:, s.slot(4), :]
                pool.wait_ge(s_idx[s.slot(4)], s.round(4) * 16 + 16)
                for j in range(2):
                    k = 2 * s.slot(2) + j
                    if not s.before(2):
                        pool.wait_ge(*used(s - 2, j))
                    pool.sem_inc(s_go, 1)
                    for t in range(TILES):
                        pool.indirect_dma_start(gath[:, k, t * width:(t + 1) * width], None, table,
                                                bass.IndirectOffsetOnAxis(ap=rows[:, j * TILES + t:j * TILES + t + 1],
                                                                          axis=0)).then_inc(s_gath[k], 16)

            def used1(s, j):
                return s_sum1, s.tick + 1

            def used2(s, j):
                return s_msg, s.tick * 2 + j + 1

            with pool.Fori(0, n_pass) as p:
                run_steps(pool, PAIRS, lambda s: gather(s, s_idx1, s_gath1, used1, xs_d, D), p)
                pool.wait_ge(s_acc1, p * PAIRS + PAIRS)

            pool.wait_ge(s_conv, CHUNKS)
            pool.memset(acc[:, :], 0.0).then_inc(s_clear, 1)
            for j in range(4):
                pool.wait_ge(s_kvt[j], 16 * chunks_in(j, 4))

            with pool.Fori(0, n_pass) as p:
                run_steps(pool, PAIRS, lambda s: gather(s, s_idx2, s_gath2, used2, kv_d, 2 * D), p)
                pool.wait_ge(s_acc2, p * PAIRS + PAIRS)

        @block.scalar
        def _(act):
            act.wait_ge(s_pre, PRE.deg)
            act.activation(dinv[:, :], dinv[:, :], ACT.Sqrt).then_inc(s_degp, 1)
            act.wait_ge(s_wts, WEIGHTS)
            act.wait_ge(s_pre, PRE.dinv)
            for b in range(XS_ACT[0], NB):
                act.activation(xs_sb[:, b, :], x_raw[:, b, :], ACT.Copy, scale=dinv[:, b:b + 1]).then_inc(s_xsa, 1)
            act.wait_ge(s_set, SET.all)
            act.wait_ge(s_xsa, NB - XS_ACT[0])
            act.wait_ge(s_pre, PRE.passes)
            n_pass = passes(act)

            def split_hi(s, mlp):
                act.wait_ge(mlp.s_x[s.slot(2)], (s.round(2) + 1) * 48)
                if not s.before(2):
                    act.wait_ge(mlp.s_l1, ((s - 2).tick + 1) * 4)
                act.activation(xsplit[0:RAD, s.slot(2), :, :], xraw[:, s.slot(2), :, :], ACT.Copy).then_inc(mlp.s_hi, 1)

            def silu(s, mlp):
                for c in range(4):
                    act.wait_ge(mlp.s_l1, s.tick * 4 + c + 1)
                    if c == 0 and not s.before(2):
                        act.wait_ge(mlp.s_w, (s - 2).tick + 1)
                    act.activation(hid[:, s.slot(2), c, :], hid_ps[c][:, :], ACT.Silu,
                                   bias=b0[:, c:c + 1]).then_inc(mlp.s_silu, 1)

            def activate(s, mlp):
                if s.before(1):
                    split_hi(s, mlp)
                    split_hi(s + 1, mlp)
                    silu(s, mlp)
                if not s.is_last(2):
                    split_hi(s + 2, mlp)
                if not s.is_last():
                    silu(s + 1, mlp)

            def sweep1(s):
                activate(s, mlp1)
                act.wait_ge(mlp1.s_w, s.tick + 1)
                if not s.before(2):
                    act.wait_ge(s_wstore[s.slot(2)], ((s - 2).round(2) + 1) * 16)
                act.activation(w_sb[:, s.slot(2), :], w_ps[:, :], ACT.Copy).then_inc(s_wcopy, 1)

            with act.Fori(0, n_pass) as p:
                run_steps(act, PAIRS, sweep1, p)
                for j in range(2):
                    act.wait_ge(s_wstore[j], (p + 1) * 16 * ((PAIRS + 1 - j) // 2))
                act.wait_ge(s_acc1, p * PAIRS + PAIRS)

            def root(c, s_var, s_std):
                act.wait_ge(s_var, c + 1)
                r = rstd[:, blocks(c)[0]:blocks(c)[-1] + 1]
                act.activation(r, r, ACT.Sqrt).then_inc(s_std, 1)

            def scaled(c, s_shift, s_norm):
                act.wait_ge(s_shift, c + 1)
                for b in blocks(c):
                    act.activation(nodes[:, b, :], nodes[:, b, :], ACT.Identity, bias=shift[:, b:b + 1],
                                   scale=rstd[:, b:b + 1]).then_inc(s_norm, 1)

            def copy_transposes(c):
                act.wait_ge(s_tr, c + 1)
                if c >= 2:
                    act.wait_ge(s_proj, blocks(c - 2)[-1] + 1)
                cols = slice(0, len(blocks(c)) * P)
                act.activation(x_t[:, c % 2, cols], bank[2 + c % 2][:, cols], ACT.Copy).then_inc(s_trc, 1)

            def q_hi(c):
                cols = slice(0, len(blocks(c)) * D)
                act.wait_ge(s_projq, c + 1)
                if c >= 4:
                    act.wait_ge(s_qt[c % 4], 48 * (c // 4 + (c % 4 == 1)))
                act.activation(q_parts[:, c % 4, 0, cols], bank[4 + c % 2][:, cols], ACT.Copy).then_inc(s_hi, 1)

            def q_mid(c):
                cols = slice(0, len(blocks(c)) * D)
                act.wait_ge(s_rest, c + 1)
                act.activation(q_parts[:, c % 4, 1, cols], q_rest[:, cols], ACT.Copy).then_inc(s_mid, 1)

            def copy_kv(c):
                if c >= 4:
                    act.wait_ge(s_kvt[c % 4], c // 4 * 16)
                for b in blocks(c)[::2]:
                    n = min(2, NB - b)
                    act.wait_ge(s_proj, b + n)
                    act.activation(kv_out[:, c % 4, b % CHUNK:b % CHUNK + n, :].rearrange("p b f -> p (b f)"),
                                   bank[6 + b // 2 % 2][:, 0:n * 2 * D], ACT.Copy).then_inc(s_projc, 1)

            root(0, s_var, s_std)
            root(1, s_var, s_std)
            scaled(0, s_shift, s_norm)
            for c in range(CHUNKS + 1):
                if c < CHUNKS:
                    copy_transposes(c)
                if c >= 1:
                    q_hi(c - 1)
                if c + 1 < CHUNKS:
                    scaled(c + 1, s_shift, s_norm)
                if c >= 1:
                    copy_kv(c - 1)
                    q_mid(c - 1)
                if c + 2 < CHUNKS:
                    root(c + 2, s_var, s_std)

            with act.Fori(0, n_pass) as p:
                run_steps(act, PAIRS, lambda s: activate(s, mlp2), p)
                act.wait_ge(s_acc2, p * PAIRS + PAIRS)

            root(0, s_fvar, s_fstd)
            root(1, s_fvar, s_fstd)
            for c in range(CHUNKS):
                scaled(c, s_fshift, s_fnorm)
                if c + 2 < CHUNKS:
                    root(c + 2, s_fvar, s_fstd)

        @block.tensor
        def _(pe):
            def count(s):
                b = s.slot(4)
                pe.wait_ge(s_hot, s.n + 1)
                for t in range(DEG_COLS):
                    one = isinstance(s.n, int)
                    mm = pe.matmul(bank[1][0:WIN, 0:HI], lo_hot[:, b, :, t], hi_hot[:, b, :, t],
                                   start=(one and s.n == 0 and t == 0),
                                   stop=(one and s.n == DEG_STEPS - 1 and t == DEG_COLS - 1),
                                   skip_group_check=True)
                mm.then_inc(s_degmm, 1)

            run_steps(pe, DEG_STEPS, count)

            pe.wait_ge(s_const, 9)
            pe.wait_ge(s_pre, PRE.viol)
            pe.matmul(bank[0][:, 0:1], ones[:, :], small[:, 2:3], start=True, stop=True).then_inc(s_viol, 1)
            pe.wait_ge(s_pre, PRE.passes)
            n_pass = passes(pe)

            pe.wait_ge(s_wts, WEIGHTS)
            pe.wait_ge(s_set, SET.all)
            pe.wait_ge(s_b1, 16)

            def layer1(s, mlp):
                b = s.slot(2)
                pe.wait_ge(mlp.s_lo, s.tick + 1)
                for c in range(4):
                    if not s.before(1):
                        pe.wait_ge(mlp.s_silu, (s - 1).tick * 4 + c + 1)
                    m, cols = c // 2, slice((c % 2) * P, (c % 2) * P + P)
                    mm = pe.matmul(hid_ps[c][:, :], w0_hi[:, m, cols], xsplit[:, b, m, :], start=True, stop=(m == 1))
                    if m == 0:
                        mm = pe.matmul(hid_ps[c][:, :], w0_lo[:, m, cols], xsplit[:, b, m, :], start=False, stop=True)
                    mm.then_inc(mlp.s_l1, 1)

            def layer2(s, mlp, s_read, per_step):
                b = s.slot(2)
                if not s.before(1):
                    pe.wait_ge(s_read, s.tick * per_step)
                pe.matmul(w_ps[:, :], ones_bf[:, :], b1_bf[:, :], start=True, stop=False, skip_group_check=True)
                for c in range(4):
                    pe.wait_ge(mlp.s_silu, s.tick * 4 + c + 1)
                    for t in range(TILES):
                        mm = pe.matmul(w_ps[:, t * D:(t + 1) * D], hid[:, b, c, t * P:(t + 1) * P], w1[:, c, :],
                                       start=False, stop=(c == 3), skip_group_check=True)
                mm.then_inc(mlp.s_w, 1)

            def sum1(s):
                b = s.slot(2)
                pe.wait_ge(s_hot1, s.tick + 1)
                if not s.before(2):
                    pe.wait_ge(s_acc1, (s - 2).tick + 1)
                for j in range(2):
                    k = 2 * b + j
                    pe.wait_ge(s_gath1[k], (s.round(2) + 1) * 16 * TILES)
                    for t in range(TILES):
                        mm = pe.matmul(sum1_ps[b][:, 0:WIN], gath[:, k, t * D:(t + 1) * D],
                                       onehot[:, b, j * TILES + t, :], start=(j == 0 and t == 0),
                                       stop=(j == 1 and t == TILES - 1))
                mm.then_inc(s_sum1, 1)

            def sweep1(s):
                if s.before(1):
                    layer1(s, mlp1)
                if not s.is_last():
                    layer1(s + 1, mlp1)
                layer2(s, mlp1, s_wcopy, 1)
                sum1(s)

            with pe.Fori(0, n_pass) as p:
                run_steps(pe, PAIRS, sweep1, p)
                pe.wait_ge(s_acc1, p * PAIRS + PAIRS)
                pe.wait_ge(s_wcopy, p * PAIRS + PAIRS)

            def convolve(c):
                if c >= 2:
                    pe.wait_ge(s_row, blocks(c - 2)[-1] + 1)
                for b in blocks(c):
                    at = b % CHUNK * D
                    mm = pe.matmul(bank[c % 2][:, at:at + D], acc[:, b * P:(b + 1) * P], w_l0_sb[:, :],
                                   start=True, stop=True, skip_group_check=True)
                mm.then_inc(s_conv, 1)

            def transpose(c):
                if c >= 2:
                    pe.wait_ge(s_trc, c - 1)
                for b in blocks(c):
                    pe.wait_ge(s_norm, b + 1)
                    at = b % CHUNK * P
                    mm = pe.transpose(bank[2 + c % 2][:, at:at + P], nodes[:, b, :], ident[:, :])
                mm.then_inc(s_tr, 1)

            def project(c):
                pe.wait_ge(s_trc, c + 1)
                if c >= 2:
                    pe.wait_ge(s_rest, c - 1)
                for b in blocks(c):
                    at = b % CHUNK * P
                    mm = pe.matmul(bank[4 + c % 2][:, at:at + D], x_t[:, c % 2, at:at + P], wqkv[:, 0:D],
                                   start=True, stop=True, skip_group_check=True)
                mm.then_inc(s_projq, 1)
                for b in blocks(c):
                    if b >= 4 and b % 2 == 0:
                        pe.wait_ge(s_projc, b // 2 - 1)
                    at, to = b % CHUNK * P, b % 2 * 2 * D
                    pe.matmul(bank[6 + b // 2 % 2][:, to:to + 2 * D], x_t[:, c % 2, at:at + P], wqkv[:, D:3 * D],
                              start=True, stop=True, skip_group_check=True).then_inc(s_proj, 1)

            convolve(0)
            convolve(1)
            for c in range(CHUNKS):
                if c + 2 < CHUNKS:
                    convolve(c + 2)
                transpose(c)
                if c >= 1:
                    project(c - 1)
            project(CHUNKS - 1)
            pe.wait_ge(s_projc, (NB + 1) // 2)

            def expand_q(s, j):
                pe.wait_ge(s_hott, s.tick * 2 + j + 1)
                if j == 0:
                    pe.wait_ge(s_qw[s.slot(2)], (s.round(2) + 1) * 48)
                if not s.before(1):
                    pe.wait_ge(s_qk, (s - 1).tick * 2 + j + 1)
                for t in range(TILES):
                    to, edges = q_ps[j][:, t * D:(t + 1) * D], slice(t * P, (t + 1) * P)
                    pe.matmul(to, onehot_t[:, j, edges], qwin[:, s.slot(2), 0, :], start=True, stop=False,
                              skip_group_check=True)
                    mm = pe.matmul(to, onehot_t[0:WIN, j, edges], qwin[0:WIN, s.slot(2), 1, :], start=False, stop=True,
                                   skip_group_check=True)
                mm.then_inc(s_q, 1)

            def sum2(s, j):
                pe.wait_ge(s_msg, s.tick * 2 + j + 1)
                if j == 0 and not s.before(1):
                    pe.wait_ge(s_acc2, s.tick)
                for t in range(TILES):
                    mm = pe.matmul(sum_ps[:, 0:WIN], msg[:, j, t, :], onehot[:, s.slot(2), j * TILES + t, :],
                                   start=(j == 0 and t == 0), stop=(j == 1 and t == TILES - 1),
                                   skip_group_check=True)
                mm.then_inc(s_sum2, 1)

            def sweep2(s):
                if s.before(1):
                    layer1(s, mlp2)
                    expand_q(s, 0)
                    expand_q(s, 1)
                if not s.is_last():
                    layer1(s + 1, mlp2)
                if not s.before(1):
                    sum2(s - 1, 1)
                layer2(s, mlp2, s_qkw, 2)
                if not s.is_last():
                    expand_q(s + 1, 0)
                sum2(s, 0)
                if not s.is_last():
                    expand_q(s + 1, 1)
                else:
                    sum2(s, 1)

            with pe.Fori(0, n_pass) as p:
                run_steps(pe, PAIRS, sweep2, p)
                pe.wait_ge(s_acc2, p * PAIRS + PAIRS)

            for c in range(CHUNKS):
                if c >= 2:
                    pe.wait_ge(s_frow, c - 1)
                for b in blocks(c):
                    at = b % CHUNK * P
                    mm = pe.transpose(bank[c % 2][:, at:at + P], acc[:, b * P:(b + 1) * P], ident[:, :])
                mm.then_inc(s_ftr, 1)

        @block.vector
        def _(dve):
            done = [0]

            def pre(ins):
                done[0] += 1
                ins.then_inc(s_pre, 1)
                return done[0]

            def pre_wait(v):
                dve.wait_ge(s_pre, v)

            def pair_bcast(row):
                return row.unsqueeze(2).to_broadcast([P, PAIRS, 2 * TILES])

            def by_pair(t):
                return t.rearrange("p (g t) -> p g t", t=2 * TILES)

            dve.wait_ge(s_const, 2)
            pre(dve.tensor_copy(iota_dig[:, :, :], iota_tmp[:, :, :]))
            dve.wait_ge(s_src, 16)
            pre(dve.tensor_scalar(dig_i[:, 0, :], src_i[:, :], WIN - 1, None, ALU.bitwise_and))
            v = pre(dve.tensor_scalar(dig_i[:, 1, :], src_i[:, :], WIN.bit_length() - 1, None, ALU.logical_shift_right))
            pre_wait(v)
            v = pre(dve.tensor_copy(dig[:, :, 0:COLS], dig_i[:, :, :]))
            pre_wait(v)

            def hots(s):
                b = s.slot(4)
                if not s.before(4):
                    dve.wait_ge(s_degmm, (s - 4).n + 1)
                for j, (hot, w) in enumerate(((lo_hot, WIN), (hi_hot, HI))):
                    digits = dig[:, j, ds(s.n * DEG_COLS, DEG_COLS)].unsqueeze(1).to_broadcast([P, w, DEG_COLS])
                    last = dve.tensor_tensor(hot[:, b, :, :], digits, iota_dig[:, 0:w, :], ALU.is_equal)
                last.then_inc(s_hot, 1)

            run_steps(dve, DEG_STEPS, hots)

            dve.wait_ge(s_set, SET.rel)
            pre(dve.tensor_reduce(small[:, 0:1], rel[:, :], AX.X, ALU.max))
            pre(dve.tensor_reduce(small[:, 1:2], rel[:, :], AX.X, ALU.min))

            dve.wait_ge(s_degmm, DEG_STEPS)
            by_half = bank[1][0:WIN, 0:HI].rearrange("p (b h) -> p h b", h=2)
            pre(dve.tensor_copy(deg[0:WIN, :], by_half[:, 0, :]))
            v = pre(dve.tensor_copy(deg[WIN:P, :], by_half[:, 1, :]))
            pre_wait(v)
            v = pre(dve.tensor_scalar(dinv[:, :], deg[:, :], 1.0, None, ALU.max))
            assert v == PRE.deg, v
            dve.wait_ge(s_degp, 1)
            v = pre(dve.reciprocal(dinv[:, :], dinv[:, :]))
            pre_wait(v)
            v = pre(dve.scalar_tensor_tensor(out=dinv[:, :], in0=deg[:, :], scalar=0.5, in1=dinv[:, :],
                                             op0=ALU.is_gt, op1=ALU.mult))
            assert v == PRE.dinv, v
            dve.wait_ge(s_wts, WEIGHTS)
            pre_wait(v)
            for j in range(2):
                own = slice(XS_DVE[j], XS_DVE[j + 1])
                v = pre(dve.tensor_tensor(xs_sb[:, own, :], x_raw[:, own, :],
                                          dinv[:, own].unsqueeze(2).to_broadcast([P, own.stop - own.start, D]),
                                          ALU.mult))
                assert v == PRE.xs + j, v

            v = pre(dve.tensor_scalar(small[:, 0:1], small[:, 0:1], WIN - 0.5, None, ALU.is_gt))
            pre_wait(v)
            v = pre(dve.scalar_tensor_tensor(out=small[:, 2:3], in0=small[:, 1:2], scalar=-0.5, in1=small[:, 0:1],
                                             op0=ALU.is_lt, op1=ALU.add))
            assert v == PRE.viol, v
            dve.wait_ge(s_viol, 1)
            v = pre(dve.tensor_scalar(small[:, 3:4], bank[0][:, 0:1], 0.5, None, ALU.is_lt))
            pre_wait(v)
            v = pre(dve.tensor_scalar(passes_i[:, :], small[0:1, 3:4], float(1 - WINDOWS), float(WINDOWS),
                                      ALU.mult, ALU.add))
            assert v == PRE.passes, v
            v = pre(dve.tensor_scalar(base_f[:, :], base_f[:, :], small[:, 3:4], None, ALU.mult))
            v_rb = pre(dve.tensor_scalar(small[0:PAIRS, 4:5], relrow0[:, 0, 0:1], small[0:PAIRS, 3:4], None, ALU.mult))
            pre_wait(v)
            pre(dve.tensor_tensor(by_pair(rel0[:, :]), by_pair(dst_f[:, :]), pair_bcast(base_f[:, :]), ALU.subtract))
            pre_wait(v_rb)
            pre(dve.tensor_scalar(relrow0[:, :, :], relrow0[:, :, :], small[0:PAIRS, 4:5], None, ALU.subtract))
            dve.wait_ge(s_const, 10)
            dve.wait_ge(s_set, SET.all)

            v = pre(dve.memset(off[:, :], 0.0))
            pre_wait(v)
            n_pass = passes(dve)

            def start_pass(p, s_pass, rows):
                steps = 4 if rows else 3
                if rows:
                    dve.tensor_scalar(relrow[:, :, :], relrow0[:, :, :], off[0:PAIRS, 0:1], None,
                                      ALU.subtract).then_inc(s_pass, 1)
                dve.tensor_scalar(base_i[:, :], base_f[0:1, :], off[0:1, 0:1], None, ALU.add).then_inc(s_pass, 1)
                dve.tensor_scalar(rel[:, :], rel0[:, :], off[:, 0:1], None, ALU.subtract).then_inc(s_pass, 1)
                dve.wait_ge(s_pass, p * steps + steps - 1)
                dve.tensor_scalar(off[:, :], off[:, :], float(WIN), None, ALU.add).then_inc(s_pass, 1)
                dve.wait_ge(s_pass, p * steps + steps)

            def one_hot(s):
                at = rel[:, ds(s.n * 2 * TILES, 2 * TILES)].unsqueeze(2).to_broadcast([P, 2 * TILES, WIN])
                nodes_in = iota_win[:, :].unsqueeze(1).to_broadcast([P, 2 * TILES, WIN])
                return dve.tensor_tensor(onehot[:, s.slot(2), :, :], at, nodes_in, ALU.is_equal)

            def split_lo(s, mlp):
                dve.wait_ge(mlp.s_hi, s.tick + 1)
                dve.tensor_tensor(xsplit[RAD:P, s.slot(2), :, :], xraw[:, s.slot(2), :, :],
                                  xsplit[0:RAD, s.slot(2), :, :].bitcast(F32), ALU.subtract).then_inc(mlp.s_lo, 1)

            bases = [None] * UNROLL

            def load_base(s):
                if isinstance(s.n, int):
                    bases[0] = dve.value_load(base_i[0:1, s.n - 1:s.n], min_val=0, max_val=NP - 1)
                elif s.c == FIRST:
                    _, bases[:] = nc.values_load_multi_w_load_instructions(
                        base_i[0:1, ds(s.n - 1, UNROLL)], engines=[mybir.EngineType.DVE], min_val=0, max_val=NP - 1,
                        skip_runtime_bounds_check_because="base_i holds node numbers")
                else:
                    bases.append(bases.pop(0))

            def add_window(s, ps, value, s_sum, s_acc):
                dve.wait_ge(s_sum, value)
                if not s.before(1):
                    dve.wait_ge(s_acc, s.tick)
                here = acc[:, ds(bases[0], WIN)]
                dve.tensor_tensor(here, here, ps[:, 0:WIN], ALU.add).then_inc(s_acc, 1)

            def sweep1(s):
                if not s.before(1):
                    load_base(s)
                if s.before(1):
                    one_hot(s).then_inc(s_hot1, 1)
                    split_lo(s, mlp1)
                    split_lo(s + 1, mlp1)
                if not s.is_last():
                    if not s.before(1):
                        dve.wait_ge(s_sum1, s.tick)
                    one_hot(s + 1).then_inc(s_hot1, 1)
                if not s.before(1):
                    add_window(s - 1, sum1_ps[(s - 1).slot(2)], s.tick, s_sum1, s_acc1)
                if not s.is_last(2):
                    split_lo(s + 2, mlp1)
                if s.is_last():
                    load_base(s + 1)
                    add_window(s, sum1_ps[s.slot(2)], s.tick + 1, s_sum1, s_acc1)

            with dve.Fori(0, n_pass) as p:
                start_pass(p, s_pass1, False)
                run_steps(dve, PAIRS, sweep1, p)
                dve.wait_ge(s_acc1, p * PAIRS + PAIRS)

            def statistics(c, row, s_row, rows_done, s_bn, s_mv):
                own = blocks(c)
                for b in range(own[0], own[-1] + 3):
                    if b in own:
                        row(b)
                    if b - 1 in own:
                        dve.wait_ge(s_row, rows_done(b - 1))
                        dve.bn_stats(stats[:, b - 1, :], nodes[:, b - 1, :]).then_inc(s_bn, 1)
                    if b - 2 in own:
                        dve.wait_ge(s_bn, b - 1)
                        dve.bn_aggr(meanvar[:, b - 2, :], stats[:, b - 2, :]).then_inc(s_mv, 1)

            def variance(c, s_mv, s_var):
                own = slice(blocks(c)[0], blocks(c)[-1] + 1)
                dve.wait_ge(s_mv, own.stop)
                dve.tensor_scalar(rstd[:, own], meanvar[:, own, 1], EPS, None, ALU.add).then_inc(s_var, 1)

            def inverse(c, s_std, s_inv):
                own = slice(blocks(c)[0], blocks(c)[-1] + 1)
                dve.wait_ge(s_std, c + 1)
                dve.reciprocal(rstd[:, own], rstd[:, own]).then_inc(s_inv, 1)

            def layer0_row(b):
                if b % CHUNK == 0:
                    dve.wait_ge(s_conv, b // CHUNK + 1)
                at = b % CHUNK * D
                dve.scalar_tensor_tensor(out=nodes[:, b, :], in0=bank[b // CHUNK % 2][:, at:at + D],
                                         scalar=dinv[:, b:b + 1], in1=nodes[:, b, :],
                                         op0=ALU.mult, op1=ALU.add).then_inc(s_row, 1)

            def scale_and_shift(c, s_std, s_inv, s_shift):
                own = slice(blocks(c)[0], blocks(c)[-1] + 1)
                inverse(c, s_std, s_inv)
                dve.wait_ge(s_inv, c + 1)
                dve.scalar_tensor_tensor(out=shift[:, own], in0=meanvar[:, own, 0], scalar=-1.0, in1=rstd[:, own],
                                         op0=ALU.mult, op1=ALU.mult).then_inc(s_shift, 1)

            def split_q(c):
                cols = slice(0, len(blocks(c)) * D)
                dve.wait_ge(s_hi, c + 1)
                if c >= 1:
                    dve.wait_ge(s_lo, c)
                dve.tensor_tensor(q_rest[:, cols], bank[4 + c % 2][:, cols], q_parts[:, c % 4, 0, cols],
                                  ALU.subtract).then_inc(s_rest, 1)
                dve.wait_ge(s_mid, c + 1)
                dve.tensor_tensor(q_parts[:, c % 4, 2, cols], q_rest[:, cols], q_parts[:, c % 4, 1, cols],
                                  ALU.subtract).then_inc(s_lo, 1)

            for c in range(2):
                statistics(c, layer0_row, s_row, lambda b: b + 1, s_bn, s_mv)
                variance(c, s_mv, s_var)
            scale_and_shift(0, s_std, s_inv, s_shift)
            for c in range(CHUNKS + 1):
                if c + 1 < CHUNKS:
                    scale_and_shift(c + 1, s_std, s_inv, s_shift)
                if c + 2 < CHUNKS:
                    statistics(c + 2, layer0_row, s_row, lambda b: b + 1, s_bn, s_mv)
                    variance(c + 2, s_mv, s_var)
                if c >= 1:
                    split_q(c - 1)
            v_off = pre(dve.memset(off[:, :], 0.0))

            def one_hot_t(s, j):
                dve.wait_ge(s_rr[s.slot(2)], (s.round(2) + 1) * 16)
                if not s.before(1):
                    dve.wait_ge(s_q, (s - 1).tick * 2 + j + 1)
                dve.tensor_scalar(onehot_t[:, j, :], relrow_sb[:, 2 * s.slot(2) + j, :], iota_part[:, :], None,
                                  ALU.is_equal).then_inc(s_hott, 1)

            def sweep2(s):
                kv = [gath[:, 2 * s.slot(2) + j, :].rearrange("p (t c f) -> p t c f", t=TILES, c=2) for j in range(2)]

                def times_k(j):
                    dve.wait_ge(s_gath2[2 * s.slot(2) + j], (s.round(2) + 1) * 16 * TILES)
                    dve.wait_ge(s_q, s.tick * 2 + j + 1)
                    dve.tensor_tensor(prod[:, j, :].rearrange("p (t f) -> p t f", t=TILES), kv[j][:, :, 0, :],
                                      q_ps[j][:, :].rearrange("p (t f) -> p t f", t=TILES), ALU.mult).then_inc(s_qk, 1)

                def times_w(j):
                    dve.wait_ge(s_qk, s.tick * 2 + j + 1)
                    if j == 0:
                        dve.wait_ge(s_wload[s.slot(2)], (s.round(2) + 1) * 16)
                        w = w_sb[:, s.slot(2), :]
                    else:
                        dve.wait_ge(mlp2.s_w, s.tick + 1)
                        w = w_ps[:, :]
                    dve.tensor_tensor(prod[:, j, :], prod[:, j, :], w, ALU.mult).then_inc(s_qkw, 1)

                def head_sums(j):
                    dve.wait_ge(s_qkw, s.tick * 2 + j + 1)
                    dve.tensor_reduce(red[:, j, :, :].rearrange("p t h -> p (t h)"),
                                      prod[:, j, :].rearrange("p (h d) -> p h d", d=HD), AX.X,
                                      ALU.add).then_inc(s_red, 1)

                def times_cutoff(j):
                    weight = cut[:, ds(s.n * 2 * TILES + j * TILES, TILES)].unsqueeze(2).to_broadcast([P, TILES, HEADS])
                    dve.wait_ge(s_red, s.tick * 2 + j + 1)
                    dve.tensor_tensor(alpha[:, j, :, :], red[:, j, :, :], weight, ALU.mult).then_inc(s_al, 1)

                def message(j):
                    a = alpha[:, j, :, :].unsqueeze(3).to_broadcast([P, TILES, HEADS, HD])
                    dve.wait_ge(s_al, s.tick * 2 + j + 1)
                    dve.tensor_tensor(msg[:, j, :, :].rearrange("p t (h d) -> p t h d", d=HD),
                                      kv[j][:, :, 1, :].rearrange("p t (h d) -> p t h d", d=HD), a,
                                      ALU.mult).then_inc(s_msg, 1)

                if s.before(1):
                    split_lo(s, mlp2)
                    split_lo(s + 1, mlp2)
                    one_hot(s)
                    one_hot_t(s, 0)
                    one_hot_t(s, 1)
                else:
                    load_base(s)
                times_k(0)
                times_k(1)
                times_w(0)
                if not s.before(1):
                    add_window(s - 1, sum_ps, s.tick * 2, s_sum2, s_acc2)
                head_sums(0)
                if not s.is_last():
                    one_hot_t(s + 1, 0)
                times_cutoff(0)
                if not s.is_last():
                    one_hot_t(s + 1, 1)
                message(0)
                if not s.is_last(2):
                    split_lo(s + 2, mlp2)
                times_w(1)
                if not s.is_last():
                    one_hot(s + 1)
                head_sums(1)
                times_cutoff(1)
                message(1)
                if s.is_last():
                    load_base(s + 1)
                    add_window(s, sum_ps, s.tick * 2 + 2, s_sum2, s_acc2)

            pre_wait(v_off)
            dve.wait_ge(s_clear, 1)
            with dve.Fori(0, n_pass) as p:
                start_pass(p, s_pass2, True)
                run_steps(dve, PAIRS, sweep2, p)
                dve.wait_ge(s_acc2, p * PAIRS + PAIRS)

            def layer1_row(b):
                if b % CHUNK == 0:
                    c = b // CHUNK
                    rows = nodes[:, b:blocks(c)[-1] + 1, :].rearrange("p b f -> p (b f)")
                    dve.wait_ge(s_ftr, c + 1)
                    dve.tensor_tensor(rows, rows, bank[c % 2][:, 0:len(blocks(c)) * D], ALU.add).then_inc(s_frow, 1)

            for c in range(CHUNKS):
                statistics(c, layer1_row, s_frow, lambda b: b // CHUNK + 1, s_fbn, s_fmv)
                variance(c, s_fmv, s_fvar)
                if c >= 1:
                    scale_and_shift(c - 1, s_fstd, s_finv, s_fshift)
            scale_and_shift(CHUNKS - 1, s_fstd, s_finv, s_fshift)


class PRE:
    deg = 9
    dinv = 11
    xs = 12
    viol = 15
    passes = 17


class SET:
    first = 1
    rel = 4
    b1 = 10
    all = 16


def _pad(a, n, fill):
    import numpy as np
    out = np.full((n,) + a.shape[1:], fill, a.dtype)
    out[:a.shape[0]] = a
    return out


def kernel(**inputs):
    import numpy as np
    import concourse.bacc as bacc
    from concourse.bass_utils import run_bass_kernel_spmd

    a = {k: np.asarray(v) for k, v in inputs.items()}
    n, e = a["x"].shape[0], a["src"].shape[0]
    groups = -(-e // GE)
    groups += groups % 2
    ep, nb = groups * GE, -(-n // P)
    src, dst = _pad(a["src"], ep, n), _pad(a["dst"], ep, n)
    cut = _pad(a["edge_weight"], ep, 0)

    def columns(v):
        return np.ascontiguousarray(v.reshape(-1, P).T)

    arrays = {
        "x": a["x"],
        "x_pad": np.ascontiguousarray(_pad(a["x"], nb * P, 0).reshape(nb, P, -1).transpose(1, 0, 2)),
        "src_idx": columns(src).reshape(P, groups, TILES),
        "src_e": columns(src),
        "dst_e": columns(dst),
        "dst_row": dst.reshape(groups, GE),
        "dst_first": np.ascontiguousarray(dst.reshape(-1, 2 * GE)[:, 0]).reshape(1, -1),
        "cut_e": columns(cut),
        "rad_t": np.ascontiguousarray(_pad(a["edge_attr_64"], ep, 0).T),
        "sph_t": np.ascontiguousarray(_pad(a["edge_attr_32"], ep, 0).T),
        "w_l0": a["L0_gnn_weight"], "b_l0": a["L0_gnn_bias"],
        "wq": a["L1_gnn_wq"], "wk": a["L1_gnn_wk"], "wv": a["L1_gnn_wv"],
    }
    for m in ("rad", "sph"):
        for w in ("w0", "b0", "w1", "b1"):
            arrays[f"{m}_{w}"] = a[f"L1_gnn_{m}_{w}"]

    nc = bacc.Bacc("TRN2", target_bir_lowering=False, num_devices=1)
    args = {k: nc.dram_tensor(f"in_{k}", v.shape, mybir.dt.from_np(v.dtype), kind="ExternalInput").ap()
            for k, v in arrays.items()}
    args["out"] = nc.dram_tensor("out_0", a["x"].shape, F32, kind="ExternalOutput").ap()
    build(nc, **args)
    r = run_bass_kernel_spmd(nc, [{f"in_{k}": v for k, v in arrays.items()}], core_ids=[0])
    return r.results[0]["out_0"]
```
